# Optimizing a Trainium2 kernel written in Bass

```python
import numpy as np
import jax
import jax.numpy as jnp

def _softmax(x, axis=-1):
    return jax.nn.softmax(x, axis=axis)

def _gelu(x):
    return jax.nn.gelu(x, approximate=True)

def _silu(x):
    return jax.nn.silu(x)

def _sigmoid(x):
    return jax.nn.sigmoid(x)

def _layernorm(x, axis=-1, eps=1e-05):
    m = jnp.mean(x, axis=axis, keepdims=True)
    v = jnp.var(x, axis=axis, keepdims=True)
    return (x - m) / jnp.sqrt(v + eps)

def _scatter_add(tgt, idx, src, axis=0):
    return tgt.at[idx].add(src)

def _segment_sum(src, seg, n):
    return jax.ops.segment_sum(src, seg, n)
kernel_name = 'mk_cond_seq_d1_seqx_r2_fe01f2'

def setup_inputs(seed: int=0):
    np.random.seed(seed)
    _w = jnp.asarray

    def _rec_inputs():
        import jax
        import jax.numpy as jnp
        _rk = jax.random.key(seed)
        x = 1.648e-05 + 1 * jax.random.normal(jax.random.fold_in(_rk, 1), (2, 2048, 512), jnp.float32)
        _lenS = 2048 - jax.random.randint(jax.random.fold_in(_rk, 7), (2,), 0, max(1, 2048 // 4) + 1, jnp.int32)
        _lenS2 = 2048 - jax.random.randint(jax.random.fold_in(_rk, 8), (2,), 0, max(1, 2048 // 4) + 1, jnp.int32)
        cond_1024 = 0.00191187 + 0.999416 * jax.random.normal(jax.random.fold_in(_rk, 11), (2, 512), jnp.float32)
        _validS = jnp.arange(2048)[None, :] < _lenS[:, None]
        _validS2 = jnp.arange(2048)[None, :] < _lenS2[:, None]
        _causal = jnp.tril(jnp.ones((2048, 2048), dtype=bool))
        mask_BxSxSx11_ik0 = jnp.where(jnp.ones((2, 2048, 2048, 11), dtype=bool), 0, 1).astype(jnp.int32)
        return (x, cond_1024, mask_BxSxSx11_ik0)
    x, cond_1024, mask_BxSxSx11_ik0 = _rec_inputs()

    def _L0_cond_setup():
        import jax, jax.numpy as jnp
        import numpy as np
        NONGT = 20
        H = 16
        NEG = -9000000000000000.0

        def _gat_attention(self_feat, cond_adj, label_bias, Wq, bq, Wk, bk, Wout, bout):
            B, N, F = self_feat.shape
            ng = min(NONGT, N)
            dh = F // H
            kv = self_feat[:, :ng]
            qh = (self_feat @ Wq.T + bq).reshape(B, N, H, dh)
            kh = (kv @ Wk.T + bk).reshape(B, ng, H, dh)
            aff = jnp.einsum('bnhd,bmhd->bnhm', qh, kh) * (1.0 / np.sqrt(dh))
            mask = cond_adj[:, :, None, :] > 0
            aff = jnp.where(mask, aff, NEG) + label_bias[:, :, None, :]
            w = jax.nn.softmax(aff, axis=-1)
            out_t = jnp.einsum('bnhm,bmf->bnhf', w, kv)
            out = jnp.einsum('bnhf,hgf->bnhg', out_t, Wout) + bout.reshape(H, F // H)
            return out.reshape(B, N, F)

        def _forward(v, q, adj, W_self, b_self, w_bias, b_bias, Wq, bq, Wk, bk, Wout, bout):
            adj_f = adj.astype(jnp.float32)
            exp_v = v
            row_zero = exp_v.sum(-1) == 0
            q_exp = jnp.where(row_zero[..., None], 0.0, q[:, None, :])
            vcq = jnp.concatenate([exp_v, q_exp], axis=-1)
            self_feat = vcq @ W_self.T + b_self
            output = self_feat
            for d in range(2):
                A = adj_f if d == 0 else jnp.swapaxes(adj_f, 1, 2)
                A = A[:, :, :NONGT, :]
                cond = A.sum(-1)
                vb = A @ w_bias + b_bias
                output = output + _gat_attention(self_feat, cond, vb, Wq[d], bq[d], Wk[d], bk[d], Wout[d], bout[d])
            rel = jax.nn.relu(output)
            return exp_v + rel
        key = jax.random.key(seed)
        ks = jax.random.split(key, 8)
        B, N, L, F, Q = (128, 36, 11, 512, 512)
        IN = F + Q
        s = 0.02
        return {'v': jax.random.normal(ks[0], (B, N, F), jnp.float32), 'q': jax.random.normal(ks[1], (B, Q), jnp.float32), 'adj': jax.random.randint(ks[2], (B, N, N, L), 0, 2, jnp.int32), 'W_self': jax.random.normal(ks[3], (F, IN), jnp.float32) * s, 'b_self': jnp.zeros((F,), jnp.float32), 'w_bias': jax.random.normal(ks[4], (L,), jnp.float32) * s, 'b_bias': jnp.zeros((), jnp.float32), 'Wq': jax.random.normal(ks[5], (2, F, F), jnp.float32) * s, 'bq': jnp.zeros((2, F), jnp.float32), 'Wk': jax.random.normal(ks[6], (2, F, F), jnp.float32) * s, 'bk': jnp.zeros((2, F), jnp.float32), 'Wout': jax.random.normal(ks[7], (2, H, F // H, F), jnp.float32) * s, 'bout': jnp.zeros((2, F), jnp.float32)}
    _L0_cond_all = _L0_cond_setup()
    _L0_cond_in = {k: v for k, v in _L0_cond_all.items() if k in ('W_self', 'b_self', 'w_bias', 'b_bias', 'Wq', 'bq', 'Wk', 'bk', 'Wout', 'bout')}
    del _L0_cond_all
    return {'x': x, 'cond_1024': cond_1024, 'mask_BxSxSx11_ik0': mask_BxSxSx11_ik0, 'L0_cond_W_self': _L0_cond_in['W_self'], 'L0_cond_b_self': _L0_cond_in['b_self'], 'L0_cond_w_bias': _L0_cond_in['w_bias'], 'L0_cond_b_bias': _L0_cond_in['b_bias'], 'L0_cond_Wq': _L0_cond_in['Wq'], 'L0_cond_bq': _L0_cond_in['bq'], 'L0_cond_Wk': _L0_cond_in['Wk'], 'L0_cond_bk': _L0_cond_in['bk'], 'L0_cond_Wout': _L0_cond_in['Wout'], 'L0_cond_bout': _L0_cond_in['bout']}

def reference(x, cond_1024, mask_BxSxSx11_ik0, L0_cond_W_self, L0_cond_b_self, L0_cond_w_bias, L0_cond_b_bias, L0_cond_Wq, L0_cond_bq, L0_cond_Wk, L0_cond_bk, L0_cond_Wout, L0_cond_bout):
    import jax
    import jax.numpy as jnp

    def _L0_cond_ref(v, q, adj, W_self, b_self, w_bias, b_bias, Wq, bq, Wk, bk, Wout, bout):
        import jax, jax.numpy as jnp
        import numpy as np
        NONGT = 20
        H = 16
        NEG = -9000000000000000.0

        def _gat_attention(self_feat, cond_adj, label_bias, Wq, bq, Wk, bk, Wout, bout):
            B, N, F = self_feat.shape
            ng = min(NONGT, N)
            dh = F // H
            kv = self_feat[:, :ng]
            qh = (self_feat @ Wq.T + bq).reshape(B, N, H, dh)
            kh = (kv @ Wk.T + bk).reshape(B, ng, H, dh)
            aff = jnp.einsum('bnhd,bmhd->bnhm', qh, kh) * (1.0 / np.sqrt(dh))
            mask = cond_adj[:, :, None, :] > 0
            aff = jnp.where(mask, aff, NEG) + label_bias[:, :, None, :]
            w = jax.nn.softmax(aff, axis=-1)
            out_t = jnp.einsum('bnhm,bmf->bnhf', w, kv)
            out = jnp.einsum('bnhf,hgf->bnhg', out_t, Wout) + bout.reshape(H, F // H)
            return out.reshape(B, N, F)

        def _forward(v, q, adj, W_self, b_self, w_bias, b_bias, Wq, bq, Wk, bk, Wout, bout):
            adj_f = adj.astype(jnp.float32)
            exp_v = v
            row_zero = exp_v.sum(-1) == 0
            q_exp = jnp.where(row_zero[..., None], 0.0, q[:, None, :])
            vcq = jnp.concatenate([exp_v, q_exp], axis=-1)
            self_feat = vcq @ W_self.T + b_self
            output = self_feat
            for d in range(2):
                A = adj_f if d == 0 else jnp.swapaxes(adj_f, 1, 2)
                A = A[:, :, :NONGT, :]
                cond = A.sum(-1)
                vb = A @ w_bias + b_bias
                output = output + _gat_attention(self_feat, cond, vb, Wq[d], bq[d], Wk[d], bk[d], Wout[d], bout[d])
            rel = jax.nn.relu(output)
            return exp_v + rel
        return _forward(v, q, adj, W_self, b_self, w_bias, b_bias, Wq, bq, Wk, bk, Wout, bout)
    x = _L0_cond_ref(x, cond_1024, mask_BxSxSx11_ik0, L0_cond_W_self, L0_cond_b_self, L0_cond_w_bias, L0_cond_b_bias, L0_cond_Wq, L0_cond_bq, L0_cond_Wk, L0_cond_bk, L0_cond_Wout, L0_cond_bout)
    return x

_drawn_inputs = setup_inputs


def setup_inputs(seed=0):
    import zlib

    import numpy as np

    out = dict(_drawn_inputs(seed))
    spreads = {'L0_cond_b_self': (0.0, 0.1),
     'L0_cond_bq': (0.0, 0.1),
     'L0_cond_bk': (0.0, 0.1),
     'L0_cond_bout': (0.0, 0.1)}
    factors = {}
    for name, (base, spread) in spreads.items():
        noise = np.random.default_rng([zlib.crc32(name.encode()), seed]).standard_normal(out[name].shape)
        drawn = base * np.exp(spread * noise) if base else spread * noise
        out[name] = jnp.asarray(drawn.astype(out[name].dtype))
    for name, factor in factors.items():
        out[name] = (out[name] * factor).astype(out[name].dtype)
    return out
```

```python
from contextlib import ExitStack

import concourse.bass as bass
from concourse import mybir

F32 = mybir.dt.float32
F32R = mybir.dt.float32r
I32 = mybir.dt.int32
ALU = mybir.AluOpType
ACT = mybir.ActivationFunctionType
AX_X = mybir.AxisListType.X

P = 128
B = 2
F = 512
H = 16
DH = F // H
NG = 20
ND = 2
L = 11
DM = ND * NG
HM = H * DM
HALF = HM // 2
KC = F // P
TPG = 4
HPG = 3
NB = (H + HPG - 1) // HPG
BK = HPG * DM
BF = HPG * DH
Z_ROW = BK
VB_Z = 2 * DM
VB_K = VB_Z + 4
NEG = -9000000000000000.0
HUGE = 3.0e38
SCALE = float(DH) ** -0.5

C_BSELF = 0
C_BQ = C_BSELF + KC
C_BK = C_BQ + ND * KC
C_Q = C_BK + ND * KC
C_WB = C_Q + KC * B
C_BB = C_WB + L
NCOLS = C_BB + 1


def build(nc, x, xT, x20, adj, wselfT, w1, wqT, wkT, woT, cols, bout, out):
    G = x.shape[0]
    GPB = G // B
    N20 = B * NG

    with ExitStack() as ctx:
        def sb(name, shape, dt=F32):
            return ctx.enter_context(nc.sbuf_tensor(name, shape, dt))

        def sem(name):
            return ctx.enter_context(nc.semaphore(name))

        def sems(name, n):
            return [sem(f"{name}{j}") for j in range(n)]

        wself_sb = sb("wself_sb", [P, 2 * KC, F])
        w1_sb = sb("w1_sb", [P, KC, F])
        wq_sb = sb("wq_sb", [P, ND, KC, F])
        wkwo_sb = sb("wkwo_sb", [P, ND, KC, F])
        cols_sb = sb("cols_sb", [P, NCOLS])
        ident = sb("ident", [P, P])
        ones = sb("ones", [P, P])
        x20_sb = sb("x20_sb", [N20, F])
        vcq = sb("vcq", [P, 2 * KC, N20 + B])
        z20 = sb("z20", [P, N20])
        s20T = sb("s20T", [P, KC, N20 + B + 1])
        keyblk = sb("keyblk", [P, ND * KC, B, 4, NG])
        qc = sb("qc", [P, ND * KC, B + 1])
        ws_hi = sb("ws_hi", [P, KC, F], F32R)
        ws_lo = sb("ws_lo", [P, KC, F], F32R)
        g_hi = sb("g_hi", [P, B, KC, HM], F32R)
        g_lo = sb("g_lo", [P, B, KC, HM], F32R)
        rep = sb("rep", [P, B, HM], F32R)
        rep_f = sb("rep_f", [P, HM])
        vblk = sb("vblk", [P, B, F])
        bout_sb = sb("bout_sb", [B + 1, ND, F])
        m_sb = sb("m_sb", [P, ND * KC, F])
        gc_hi = wq_sb[0:B + 1, 0, :, :].rearrange("p a b -> p (a b)")[:, 0:B * HM]\
            .rearrange("p (b n) -> p b n", b=B)
        gc_lo = wq_sb[0:B + 1, 1, :, :].rearrange("p a b -> p (a b)")[:, 0:B * HM]\
            .rearrange("p (b n) -> p b n", b=B)
        v_sb = w1_sb[0:N20, 0:ND, :]
        crow = w1_sb[0:B + 1, ND, :]
        m_flat = m_sb[:, :, :].rearrange("p a b -> p (a b)")
        logit = m_flat[:, 0:HM]
        expd = m_flat[:, HM:2 * HM]
        wT = m_flat[:, 2 * HM:2 * HM + NB * P]
        outb = m_flat[:, 2 * HM + NB * P:2 * HM + NB * P + 2 * F].rearrange("p (s n) -> p s n", s=2)

        xT_sb = sb("xT_sb", [P, TPG, KC, P])
        xh = sb("xh", [P, TPG, KC, P], F32R)
        xl = sb("xl", [P, TPG, KC, P], F32R)
        x_sb = sb("x_sb", [P, TPG, F])
        rowsum = sb("rowsum", [P, TPG])
        rs_junk = sb("rs_junk", [P, F])
        adj_sb = sb("adj_sb", [P, TPG, L, DM], I32)
        vb = sb("vb", [P, TPG, DM])
        cond = sb("cond", [P, TPG, DM])
        negvb = sb("negvb", [P, TPG, DM])
        cap_next = sb("cap_next", [P, TPG, DM])
        cap = sb("cap", [P, TPG, DM])
        vbn = sb("vbn", [P, TPG, P])
        vbT = sb("vbT", [P, 2, P], F32R)
        mx = sb("mx", [P, H * ND])
        den = sb("den", [P, H * ND])
        rden = sb("rden", [P, H * ND])
        w = sb("w", [P, NB, P])

        def ps(name, shape):
            return ctx.enter_context(nc.psum_tensor(name, shape, F32))

        lgP = ps("lgP", [P, 2, 512])
        outP = [ps("outP0", [P, 512]), ps("outP1", [P, 512])]
        trP = ps("trP", [P, 2, 512])
        auxP = [ps("auxP0", [P, 512]), ps("auxP1", [P, 512])]
        foldP = [lgP[:, 0, :], lgP[:, 1, :], outP[0][:, :], outP[1][:, :]]

        x20_in, cols_in, w1_in, bout_in = sem("x20_in"), sem("cols_in"), sem("w1_in"), sem("bout_in")
        wself_in = sems("wself_in", 2)
        wq_in, wk_in, wo_in = sems("wq_in", ND), sem("wk_in"), sem("wo_in")
        consts_ready, keyblk_zeroed, bout_zeroed = sem("consts_ready"), sem("keyblk_zeroed"), sem("bout_zeroed")
        vbn_set, w_set, vblk_zeroed = sem("vbn_set"), sem("w_set"), sem("vblk_zeroed")
        x20T_done, vcqx_ready, sum20_done, z20_ready, vcq_ready = (
            sem("x20T_done"), sem("vcqx_ready"), sem("sum20_done"), sem("z20_ready"), sem("vcq_ready"))
        s20_done, s20_ready = sem("s20_done"), sem("s20_ready")
        m_done, m_ready = sem("m_done"), sem("m_ready")
        k_done, key_ready, qc_done, qc_ready = sem("k_done"), sem("key_ready"), sem("qc_done"), sem("qc_ready")
        fold_done, fold_hi, fold_lo = sem("fold_done"), sem("fold_hi"), sem("fold_lo")
        v_done, v_ready, crow_done, crow_ready = sem("v_done"), sem("v_ready"), sem("crow_done"), sem("crow_ready")
        vblk_in, rep_in, rep_ready, rep_step = sem("vblk_in"), sem("rep_in"), sem("rep_ready"), sem("rep_step")
        ws_hi_ready, ws_lo_ready = sem("ws_hi_ready"), sem("ws_lo_ready")
        vb01_done, vb01_ready, vbT_ready = sem("vb01_done"), sem("vb01_ready"), sem("vbT_ready")
        vbtr_done = sem("vbtr_done")

        xT_in, x_in = sems("xT_in", TPG), sems("x_in", TPG)
        adj_in, adj_used = sem("adj_in"), sem("adj_used")
        xh_ready, xl_ready, rowsum_ready, z_ready = sem("xh_ready"), sem("xl_ready"), sem("rowsum_ready"), sem("z_ready")
        vb_step, vb_ready, cap_ready = sem("vb_step"), sem("vb_ready"), sem("cap_ready")
        lg_done, self_done = sem("lg_done"), sems("self_done", TPG)
        masked, max_ready, shifted, exp_ready = sem("masked"), sem("max_ready"), sem("shifted"), sem("exp_ready")
        den_ready, rden_ready, w_ready = sem("den_ready"), sem("rden_ready"), sem("w_ready")
        tr_done, tr_copied = sem("tr_done"), sem("tr_copied")
        pv_done, fin_ready, stored = sem("pv_done"), sem("fin_ready"), sems("stored", 2)

        W_STEPS = 3
        TR_COPIES = 2
        VB_STEPS = L + 4

        def slot_of(i, k):
            return i + k // TPG, k % TPG

        def free(eng, s, n):
            if not (isinstance(n, int) and n <= 0):
                eng.wait_ge(s, n)

        block = ctx.enter_context(nc.Block())

        @block.sync
        def _(sp):
            sp.dma_start(x20_sb[:, :], x20).then_inc(x20_in, 16)
            sp.dma_start(cols_sb[:, :], cols).then_inc(cols_in, 16)
            for half in range(2):
                sp.dma_start(wself_sb[:, half * KC:(half + 1) * KC, :],
                             wselfT[half * F:(half + 1) * F, :].rearrange("(c p) n -> p c n", p=P))\
                    .then_inc(wself_in[half], 16)
            sp.dma_start(w1_sb[:, :, :], w1.rearrange("(c p) n -> p c n", p=P)).then_inc(w1_in, 16)
            for d in range(ND):
                sp.dma_start(wq_sb[:, d, :, :], wqT[d].rearrange("(c p) n -> p c n", p=P)).then_inc(wq_in[d], 16)
            for d in range(ND):
                sp.dma_start(wkwo_sb[:, d, :, :], wkT[d].rearrange("(c p) n -> p c n", p=P)).then_inc(wk_in, 16)
            sp.dma_start(adj_sb[:, :, :, :], adj[0]).then_inc(adj_in, 16)
            for k in range(2):
                sp.dma_start(xT_sb[:, k, :, :], xT[0, k]).then_inc(xT_in[k], 16)
                sp.dma_start(x_sb[:, k, :], x[0, k]).then_inc(x_in[k], 16)
            sp.wait_ge(bout_zeroed, 1)
            sp.dma_start(bout_sb[B:B + 1, :, :], bout).then_inc(bout_in, 16)
            sp.wait_ge(k_done, 1)
            for d in range(ND):
                sp.dma_start(wkwo_sb[:, d, :, :], woT[d].rearrange("(c p) n -> p c n", p=P)).then_inc(wo_in, 16)
            for k in range(2, TPG):
                sp.dma_start(xT_sb[:, k, :, :], xT[0, k]).then_inc(xT_in[k], 16)
                sp.dma_start(x_sb[:, k, :], x[0, k]).then_inc(x_in[k], 16)
            sp.wait_ge(fold_hi, KC * (KC + 1))
            sp.wait_ge(fold_lo, KC * (KC + 1))
            sp.wait_ge(rep_ready, 2)
            for b in range(B):
                for r, src in enumerate((gc_hi[b:b + 1, b, :], gc_lo[b:b + 1, b, :],
                                         gc_hi[B:B + 1, b, :], gc_lo[B:B + 1, b, :])):
                    sp.dma_start(rep[VB_Z + r:VB_Z + r + 1, b, :].bitcast(F32), src).then_inc(rep_in, 16)
            sp.wait_ge(v_ready, ND)
            sp.wait_ge(vblk_zeroed, 1)
            for b in range(B):
                for d in range(ND):
                    for j in range(HPG):
                        r = slice(j * DM + d * NG, j * DM + (d + 1) * NG)
                        sp.dma_start(vblk[r, b, :].rearrange("p (h n) -> p h n", n=DH)[:, j::HPG, :],
                                     v_sb[b * NG:(b + 1) * NG, d, :].rearrange("p (h n) -> p h n", n=DH)[:, j::HPG, :])\
                            .then_inc(vblk_in, 16)
            sp.wait_ge(crow_ready, 2)
            for b in range(B):
                sp.dma_start(vblk[Z_ROW:Z_ROW + 1, b, :], crow[b:b + 1, :]).then_inc(vblk_in, 16)
                sp.dma_start(vblk[Z_ROW + 1:Z_ROW + 2, b, :], crow[B:B + 1, :]).then_inc(vblk_in, 16)

            def turn(i, last):
                if not last:
                    sp.wait_ge(adj_used, i + 1)
                    sp.dma_start(adj_sb[:, :, :, :], adj[i + 1]).then_inc(adj_in, 16)
                for k in range(TPG):
                    if not last:
                        sp.wait_ge(xl_ready, TPG * i + k + 1)
                        sp.dma_start(xT_sb[:, k, :, :], xT[i + 1, k]).then_inc(xT_in[k], 16)
                    sp.wait_ge(fin_ready, TPG * i + k + 1)
                    sp.dma_start(out[i, k], outb[:, k % 2, :]).then_inc(stored[k % 2], 16)
                    if not last:
                        sp.dma_start(x_sb[:, k, :], x[i + 1, k]).then_inc(x_in[k], 16)

            turn(0, False)
            with sp.Fori(1, G - 1) as i:
                turn(i, False)
            turn(G - 1, True)
            for s in range(2):
                sp.wait_ge(stored[s], 16 * G * TPG // 2)

        @block.tensor
        def _(pe):
            def mm(o, a, b, start, stop):
                return nc.tensor.matmul(o, a, b, start=start, stop=stop, skip_group_check=True)

            pe.wait_ge(x20_in, 16)
            pe.wait_ge(consts_ready, 3)
            for c in range(KC):
                last = nc.tensor.transpose(auxP[0][:, c * N20:(c + 1) * N20], x20_sb[:, c * P:(c + 1) * P],
                                           ident[0:N20, 0:N20])
            last.then_inc(x20T_done, 1)
            pe.wait_ge(vcqx_ready, 2)
            for c in range(KC):
                last = mm(auxP[1][:, 0:N20], ones[:, :], vcq[:, c, 0:N20], c == 0, c == KC - 1)
            last.then_inc(sum20_done, 1)
            pe.wait_ge(vcq_ready, 2)
            pe.wait_ge(wself_in[0], 16)
            pe.wait_ge(wself_in[1], 16)
            for f in range(KC):
                for c in range(2 * KC):
                    last = mm(trP[:, 0, f * 64:f * 64 + N20 + B], wself_sb[:, c, f * P:(f + 1) * P],
                              vcq[:, c, :], c == 0, c == 2 * KC - 1)
            last.then_inc(s20_done, 1)
            pe.wait_ge(w1_in, 16)
            for d in range(ND):
                pe.wait_ge(wq_in[d], 16)
                for c in range(KC):
                    n = d * KC + c
                    if n >= 4:
                        pe.wait_ge(m_ready, n - 3)
                    for f in range(KC):
                        last = mm(foldP[n % 4], wq_sb[:, d, f, c * P:(c + 1) * P], w1_sb[:, f, :], f == 0, f == KC - 1)
                    last.then_inc(m_done, 1)
            pe.wait_ge(s20_ready, 3)
            pe.wait_ge(wk_in, 16 * ND)
            for d in range(ND):
                for c in range(KC):
                    n = d * KC + c
                    for f in range(KC):
                        last = mm(trP[:, 1, n * N20:(n + 1) * N20], wkwo_sb[:, d, f, c * P:(c + 1) * P],
                                  s20T[:, f, 0:N20], f == 0, f == KC - 1)
            last.then_inc(k_done, 1)
            for d in range(ND):
                for c in range(KC):
                    n = d * KC + c
                    for f in range(KC):
                        last = mm(auxP[0][:, n * 4:n * 4 + B + 1], wq_sb[:, d, f, c * P:(c + 1) * P],
                                  s20T[:, f, N20:N20 + B + 1], f == 0, f == KC - 1)
            last.then_inc(qc_done, 1)
            for f in range(KC):
                last = nc.tensor.transpose(auxP[1][0:B + 1, f * P:(f + 1) * P], s20T[:, f, N20:N20 + B + 1], ident[:, :])
            last.then_inc(crow_done, 1)
            pe.wait_ge(m_ready, ND * KC)
            pe.wait_ge(key_ready, 4)
            pe.wait_ge(qc_ready, 2)
            n = 0
            for c in range(KC):
                for ic in range(KC + 1):
                    if n >= 4:
                        pe.wait_ge(fold_hi, n - 3)
                        pe.wait_ge(fold_lo, n - 3)
                    for d in range(ND):
                        if ic < KC:
                            o, a = foldP[n % 4], m_sb[:, d * KC + c, ic * P:(ic + 1) * P]
                        else:
                            o, a = foldP[n % 4][0:B + 1], qc[:, d * KC + c, :]
                        o = o[:, 0:B * 4 * DM].rearrange("p (b h n) -> p b h n", b=B, h=4)[:, :, :, d * NG:(d + 1) * NG]
                        last = mm(o, a, keyblk[:, d * KC + c, :, :, :], d == 0, d == 1)
                    last.then_inc(fold_done, 1)
                    n += 1
            pe.wait_ge(wo_in, 16 * ND)
            pe.wait_ge(crow_ready, 2)
            for d in range(ND):
                for f in range(KC):
                    last = mm(auxP[d][0:N20, :], s20T[:, f, 0:N20], wkwo_sb[:, d, f, :], f == 0, f == KC - 1)
                last.then_inc(v_done, 1)
            pe.wait_ge(vb_ready, 1)
            pe.wait_ge(z_ready, 2)
            for k in range(2):
                last = nc.tensor.transpose(trP[:, 1, k * P:(k + 1) * P], vbn[:, k, :], ident[:, :])
            last.then_inc(vb01_done, 1)

            def logits(i, k, b, first=False):
                t = TPG * i + k
                pe.wait_ge(xh_ready, t + 1)
                pe.wait_ge(xl_ready, t + 1)
                free(pe, masked, t)
                if not first:
                    free(pe, vbT_ready, t - 1)
                s = k % TPG
                for c in range(KC):
                    for a, g in ((xh, g_hi), (xh, g_lo), (xl, g_hi)):
                        for h in range(2):
                            mm(lgP[:, h, 0:HALF], a[:, s, c, :], g[:, b, c, h * HALF:(h + 1) * HALF],
                               c == 0 and a is xh and g is g_hi, False)
                for h in range(2):
                    last = mm(lgP[:, h, 0:HALF], vbT[0:VB_K, k % 2, :], rep[0:VB_K, b, h * HALF:(h + 1) * HALF],
                              False, True)
                last.then_inc(lg_done, 1)

            def self_rows(i, k, first=False):
                t = TPG * i + k
                if not first:
                    free(pe, fin_ready, t - 1)
                s = k % TPG
                for c in range(KC):
                    for a, g in ((xh, ws_hi), (xh, ws_lo), (xl, ws_hi)):
                        last = mm(outP[k % 2][:, :], a[:, s, c, :], g[:, c, :],
                                  c == 0 and a is xh and g is ws_hi, False)
                last.then_inc(self_done[s], 1)

            def turned(i, k):
                t = TPG * i + k
                pe.wait_ge(w_ready, W_STEPS * t + W_STEPS)
                free(pe, tr_copied, TR_COPIES * t)
                for e in range(NB):
                    last = nc.tensor.transpose(trP[:, e // 4, (e % 4) * P:(e % 4 + 1) * P], w[:, e, :], ident[:, :])
                last.then_inc(tr_done, 1)

            def turned_vb(i, k):
                t = TPG * i + k
                i2, s2 = slot_of(i, k)
                free(pe, vbT_ready, t - 2)
                pe.wait_ge(vb_ready, i2 + 1)
                pe.wait_ge(z_ready, t + 1)
                nc.tensor.transpose(auxP[0][:, 0:P], vbn[:, s2, :], ident[:, :]).then_inc(vbtr_done, 1)

            def values(i, k, b):
                t = TPG * i + k
                pe.wait_ge(tr_copied, TR_COPIES * t + TR_COPIES)
                for e in range(NB):
                    n = min(BF, F - e * BF)
                    last = mm(outP[k % 2][:, e * BF:e * BF + n], wT[:, e * P:(e + 1) * P],
                              vblk[:, b, e * BF:e * BF + n], False, e == NB - 1)
                last.then_inc(pv_done, 1)

            pe.wait_ge(ws_hi_ready, 1)
            pe.wait_ge(ws_lo_ready, 1)
            pe.wait_ge(fold_hi, KC * (KC + 1))
            pe.wait_ge(fold_lo, KC * (KC + 1))
            pe.wait_ge(rep_in, 16 * 4 * B)
            pe.wait_ge(vb01_ready, 1)
            logits(0, 0, 0, first=True)
            self_rows(0, 0, first=True)
            pe.wait_ge(vblk_in, 16 * (B * ND * HPG + 2 * B))

            def turn(i, last):
                b = i // GPB
                for k in range(TPG):
                    more = not (last and k == TPG - 1)
                    if more:
                        i1, _ = slot_of(i, k + 1)
                        logits_next = (i, k + 1) if k + 1 < TPG else (i + 1, 0)
                        logits(*logits_next, logits_next[0] // GPB)
                    turned(i, k)
                    if more:
                        self_rows(*logits_next)
                    if not (last and k >= TPG - 2):
                        turned_vb(i, k + 2)
                    values(i, k, b)

            turn(0, False)
            with pe.Fori(1, G - 1) as i:
                turn(i, False)
            turn(G - 1, True)

        @block.scalar
        def _(act):
            def split_hi(i, k):
                i2, s = slot_of(i, k)
                act.wait_ge(xT_in[s], 16 * i2 + 16)
                free(act, self_done[s], i2)
                nc.scalar.activation(xh[:, s, :, :], xT_sb[:, s, :, :], ACT.Copy).then_inc(xh_ready, 1)
                act.wait_ge(x_in[s], 16 * i2 + 16)
                free(act, rowsum_ready, TPG * i + k)
                nc.scalar.activation(rs_junk[:, :], x_sb[:, s, :], ACT.Copy,
                                     accum_out=rowsum[:, s:s + 1]).then_inc(rowsum_ready, 1)

            act.wait_ge(wself_in[0], 16)
            nc.scalar.activation(ws_hi[:, :, :], wself_sb[:, 0:KC, :], ACT.Copy).then_inc(ws_hi_ready, 1)
            for n in range(ND * KC):
                act.wait_ge(m_done, n + 1)
                nc.scalar.activation(m_sb[:, n, :], foldP[n % 4], ACT.Copy).then_inc(m_ready, 1)
            split_hi(0, 0)
            split_hi(0, 1)
            n = 0
            for c in range(KC):
                for ic in range(KC + 1):
                    act.wait_ge(fold_done, n + 1)
                    if ic < KC:
                        o, a = g_hi[:, :, ic, :], foldP[n % 4]
                    else:
                        o, a = gc_hi, foldP[n % 4][0:B + 1]
                    nc.scalar.activation(o[:, :, c * 4 * DM:(c + 1) * 4 * DM].bitcast(F32R),
                                         a[:, 0:B * 4 * DM].rearrange("p (b n) -> p b n", b=B),
                                         ACT.Copy, scale=SCALE).then_inc(fold_hi, 1)
                    n += 1
            for d in range(ND):
                act.wait_ge(v_done, d + 1)
                nc.scalar.activation(v_sb[:, d, :], auxP[d][0:N20, :], ACT.Copy).then_inc(v_ready, 1)
            act.wait_ge(vb01_done, 1)
            nc.scalar.activation(vbT[:, :, :], trP[:, 1, 0:2 * P].rearrange("p (s n) -> p s n", s=2), ACT.Copy)\
                .then_inc(vb01_ready, 1)

            def turn(i, last):
                for k in range(TPG):
                    t = TPG * i + k
                    ahead = not (last and k >= TPG - 2)
                    if ahead:
                        split_hi(i, k + 2)
                    act.wait_ge(shifted, t + 1)
                    free(act, w_ready, W_STEPS * t)
                    nc.scalar.activation(expd, logit, ACT.Exp).then_inc(exp_ready, 1)
                    act.wait_ge(tr_done, t + 1)
                    free(act, pv_done, t)
                    nc.scalar.activation(wT[:, 0:4 * P], trP[:, 0, :], ACT.Copy).then_inc(tr_copied, 1)
                    nc.scalar.activation(wT[:, 4 * P:NB * P], trP[:, 1, 0:2 * P], ACT.Copy).then_inc(tr_copied, 1)
                    if ahead:
                        act.wait_ge(vbtr_done, t + 1)
                        act.wait_ge(lg_done, t + 1)
                        nc.scalar.activation(vbT[:, k % 2, :], auxP[0][:, 0:P], ACT.Copy).then_inc(vbT_ready, 1)

            turn(0, False)
            with act.Fori(1, G - 1) as i:
                turn(i, False)
            turn(G - 1, True)

        @block.vector
        def _(dve):
            nc.vector.memset(vcq[:, 0:KC, N20:N20 + B], 0.0).then_inc(vcqx_ready, 1)
            nc.vector.memset(keyblk[:, :, :, :, :], 0.0).then_inc(keyblk_zeroed, 1)
            dve.wait_ge(x20T_done, 1)
            nc.vector.tensor_copy(vcq[:, 0:KC, 0:N20], auxP[0][:, 0:KC * N20].rearrange("p (c n) -> p c n", c=KC))\
                .then_inc(vcqx_ready, 1)
            dve.wait_ge(sum20_done, 1)
            nc.vector.tensor_scalar(z20[:, :], auxP[1][:, 0:N20], 0.0, None, ALU.not_equal).then_inc(z20_ready, 1)
            dve.wait_ge(cols_in, 16)
            q_cols = cols_sb[:, C_Q:C_Q + KC * B].rearrange("p (c b) -> p c b", b=B)
            dve.wait_ge(z20_ready, 1)
            nc.vector.tensor_tensor(
                vcq[:, KC:2 * KC, 0:N20].rearrange("p c (b m) -> p c b m", b=B),
                z20[:, :].rearrange("p (b m) -> p b m", b=B).unsqueeze(1).to_broadcast([P, KC, B, NG]),
                q_cols.unsqueeze(3).to_broadcast([P, KC, B, NG]), ALU.mult).then_inc(vcq_ready, 1)
            nc.vector.tensor_copy(vcq[:, KC:2 * KC, N20:N20 + B], q_cols).then_inc(vcq_ready, 1)
            dve.wait_ge(ws_hi_ready, 1)
            nc.vector.tensor_tensor(ws_lo[:, :, :], wself_sb[:, 0:KC, :], ws_hi[:, :, :].bitcast(F32), ALU.subtract)\
                .then_inc(ws_lo_ready, 1)
            b_self = cols_sb[:, C_BSELF:C_BSELF + KC]
            dve.wait_ge(s20_done, 1)
            s20P = trP[:, 0, 0:KC * 64].rearrange("p (c n) -> p c n", c=KC)
            nc.vector.tensor_tensor(s20T[:, :, 0:N20], s20P[:, :, 0:N20],
                                    b_self.unsqueeze(2).to_broadcast([P, KC, N20]), ALU.add).then_inc(s20_ready, 1)
            nc.vector.tensor_copy(s20T[:, :, N20:N20 + B], s20P[:, :, N20:N20 + B]).then_inc(s20_ready, 1)
            nc.vector.tensor_copy(s20T[:, :, N20 + B:N20 + B + 1], b_self.unsqueeze(2)).then_inc(s20_ready, 1)

            adj_l = [adj_sb[:, :, j, :] for j in range(L)]
            w_bias = [cols_sb[:, C_WB + j:C_WB + j + 1] for j in range(L)]

            def link(ins, i, step):
                ins.then_inc(vb_step, 1)
                dve.wait_ge(vb_step, VB_STEPS * i + step)

            def edge_bias(i, part):
                if part == 0:
                    dve.wait_ge(adj_in, 16 * i + 16)
                    link(nc.vector.tensor_scalar(vb[:, :, :], adj_l[0], w_bias[0], cols_sb[:, C_BB:C_BB + 1],
                                                 ALU.mult, ALU.add), i, 1)
                for j in (range(1, 6) if part == 0 else range(6, L)):
                    link(nc.vector.scalar_tensor_tensor(vb[:, :, :], adj_l[j], w_bias[j], vb[:, :, :],
                                                        ALU.mult, ALU.add), i, j + 1)

            def edge_rows(i):
                link(nc.vector.tensor_copy(vbn[:, :, 0:DM].bitcast(F32R), vb[:, :, :]), i, L + 1)
                nc.vector.tensor_tensor(vbn[:, :, DM:2 * DM].bitcast(F32R), vb[:, :, :], vbn[:, :, 0:DM],
                                        ALU.subtract).then_inc(vb_ready, 1)

            def edge_cap(i):
                ins = nc.vector.tensor_reduce(cond[:, :, :], adj_sb[:, :, :, :].rearrange("p t l m -> p t m l"),
                                              AX_X, ALU.add)
                link(ins, i, L + 2)
                link(nc.vector.tensor_scalar(cap_next[:, :, :], cond[:, :, :], 0.0, HUGE, ALU.is_gt, ALU.mult), i, L + 3)
                nc.vector.tensor_scalar(negvb[:, :, :], vb[:, :, :], NEG, None, ALU.add).then_inc(adj_used, 1)

            def edge_cap_in(i):
                dve.wait_ge(adj_used, i + 1)
                link(nc.vector.tensor_tensor(negvb[:, :, :], negvb[:, :, :], cap_next[:, :, :], ALU.add), i, L + 4)
                nc.vector.tensor_copy(cap[:, :, :], negvb[:, :, :]).then_inc(cap_ready, 1)

            def row_flags(i, k):
                i2, s = slot_of(i, k)
                dve.wait_ge(rowsum_ready, TPG * i + k + 1)
                nc.vector.tensor_scalar(vbn[:, s, VB_Z:VB_Z + 2], rowsum[:, s:s + 1].to_broadcast([P, 2]),
                                        0.0, None, ALU.not_equal).then_inc(z_ready, 1)

            def shift(i, k):
                t = TPG * i + k
                dve.wait_ge(lg_done, t + 1)
                dve.wait_ge(cap_ready, i + 1)
                nc.vector.tensor_tensor(
                    logit.rearrange("p (a h n) -> p a h n", a=2, n=DM),
                    lgP[:, :, 0:HALF].rearrange("p a (h n) -> p a h n", n=DM),
                    cap[:, k, :].unsqueeze(1).unsqueeze(1).to_broadcast([P, 2, H // 2, DM]),
                    ALU.min).then_inc(masked, 1)
                dve.wait_ge(masked, t + 1)
                soft = logit.rearrange("p (g m) -> p g m", m=NG)
                nc.vector.tensor_reduce(mx[:, :], soft, AX_X, ALU.max).then_inc(max_ready, 1)
                dve.wait_ge(max_ready, t + 1)
                nc.vector.tensor_tensor(soft, soft, mx[:, :].unsqueeze(2).to_broadcast([P, H * ND, NG]),
                                        ALU.subtract).then_inc(shifted, 1)

            def weigh(i, k):
                t = TPG * i + k
                dve.wait_ge(exp_ready, t + 1)
                nc.vector.tensor_reduce(den[:, :], expd.rearrange("p (g m) -> p g m", m=NG), AX_X, ALU.add)\
                    .then_inc(den_ready, 1)
                dve.wait_ge(den_ready, t + 1)
                nc.vector.reciprocal(rden[:, :], den[:, :]).then_inc(rden_ready, 1)
                dve.wait_ge(rden_ready, t + 1)
                free(dve, tr_done, t)
                full = (NB - 1) * BK
                nf = full // NG
                nc.vector.tensor_tensor(
                    w[:, 0:NB - 1, 0:BK].rearrange("p e (g m) -> p e g m", m=NG),
                    expd[:, 0:full].rearrange("p (e g m) -> p e g m", e=NB - 1, m=NG),
                    rden[:, 0:nf].rearrange("p (e g) -> p e g", e=NB - 1).unsqueeze(3)
                    .to_broadcast([P, NB - 1, BK // NG, NG]), ALU.mult).then_inc(w_ready, 1)
                nc.vector.tensor_tensor(
                    w[:, NB - 1, 0:HM - full].rearrange("p (g m) -> p g m", m=NG),
                    expd[:, full:HM].rearrange("p (g m) -> p g m", m=NG),
                    rden[:, nf:].unsqueeze(2).to_broadcast([P, H * ND - nf, NG]), ALU.mult).then_inc(w_ready, 1)
                nc.vector.tensor_scalar(w[:, :, Z_ROW:Z_ROW + 1], rowsum[:, k:k + 1].unsqueeze(1)
                                        .to_broadcast([P, NB, 1]), 0.0, None, ALU.not_equal).then_inc(w_ready, 1)

            def finish(i, k):
                t = TPG * i + k
                dve.wait_ge(pv_done, t + 1)
                dve.wait_ge(x_in[k], 16 * i + 16)
                free(dve, stored[k % 2], 16 * (2 * i + k // 2))
                nc.vector.scalar_tensor_tensor(outb[:, k % 2, :], outP[k % 2][:, :], 0.0, x_sb[:, k, :],
                                               ALU.max, ALU.add).then_inc(fin_ready, 1)

            edge_bias(0, 0)
            edge_bias(0, 1)
            dve.wait_ge(vbn_set, 2)
            edge_rows(0)
            edge_cap(0)
            edge_cap_in(0)
            b_k = cols_sb[:, C_BK:C_BK + ND * KC]
            kP = trP[:, 1, 0:ND * KC * N20].rearrange("p (c b m) -> p c b m", b=B, m=NG)
            dve.wait_ge(k_done, 1)
            dve.wait_ge(keyblk_zeroed, 1)
            for h in range(4):
                r = slice(h * DH, (h + 1) * DH)
                nc.vector.tensor_tensor(keyblk[r, :, :, h, :], kP[r],
                                        b_k[r].unsqueeze(2).unsqueeze(2).to_broadcast([DH, ND * KC, B, NG]),
                                        ALU.add).then_inc(key_ready, 1)
            dve.wait_ge(qc_done, 1)
            qcP = auxP[0][:, 0:ND * KC * 4].rearrange("p (c n) -> p c n", n=4)
            nc.vector.tensor_copy(qc[:, :, 0:B], qcP[:, :, 0:B]).then_inc(qc_ready, 1)
            nc.vector.tensor_tensor(qc[:, :, B:B + 1], qcP[:, :, B:B + 1],
                                    cols_sb[:, C_BQ:C_BQ + ND * KC].unsqueeze(2), ALU.add).then_inc(qc_ready, 1)
            dve.wait_ge(crow_done, 1)
            dve.wait_ge(bout_in, 16)
            nc.vector.tensor_tensor(crow, auxP[1][0:B + 1, :], bout_sb[:, 0, :], ALU.add).then_inc(crow_ready, 1)
            dve.wait_ge(crow_ready, 1)
            nc.vector.tensor_tensor(crow, crow, bout_sb[:, 1, :], ALU.add).then_inc(crow_ready, 1)
            row_flags(0, 0)
            row_flags(0, 1)
            n = 0
            for c in range(KC):
                for ic in range(KC + 1):
                    dve.wait_ge(fold_hi, n + 1)
                    if ic < KC:
                        o, hi, a = g_lo[:, :, ic, :], g_hi[:, :, ic, :], foldP[n % 4]
                    else:
                        o, hi, a = gc_lo, gc_hi, foldP[n % 4][0:B + 1]
                    s = slice(c * 4 * DM, (c + 1) * 4 * DM)
                    nc.vector.scalar_tensor_tensor(o[:, :, s].bitcast(F32R),
                                                   a[:, 0:B * 4 * DM].rearrange("p (b n) -> p b n", b=B),
                                                   SCALE, hi[:, :, s].bitcast(F32), ALU.mult, ALU.subtract)\
                        .then_inc(fold_lo, 1)
                    n += 1
            shift(0, 0)
            dve.wait_ge(w_set, 2)
            weigh(0, 0)

            def turn(i, last):
                for k in range(TPG):
                    more = not (last and k == TPG - 1)
                    if k == TPG - 1 and not last:
                        edge_cap_in(i + 1)
                    if more:
                        i1, k1 = (i, k + 1) if k + 1 < TPG else (i + 1, 0)
                        shift(i1, k1)
                    if not (last and k >= TPG - 2):
                        row_flags(i, k + 2)
                    if not last and k == 0:
                        edge_bias(i + 1, 0)
                    if not last and k == 1:
                        edge_bias(i + 1, 1)
                    if not last and k == 2:
                        dve.wait_ge(vbtr_done, TPG * i + 2)
                        edge_rows(i + 1)
                        edge_cap(i + 1)
                    if more:
                        weigh(i1, k1)
                    finish(i, k)

            turn(0, False)
            with dve.Fori(1, G - 1) as i:
                turn(i, False)
            turn(G - 1, True)

        @block.gpsimd
        def _(pool):
            nc.gpsimd.memset(ident[:, :], 0.0).then_inc(consts_ready, 1)
            nc.gpsimd.memset(ones[:, :], 1.0).then_inc(consts_ready, 1)
            pool.wait_ge(consts_ready, 1)
            nc.gpsimd.affine_select(out=ident[:, :], in_=ident[:, :], compare_op=ALU.not_equal, fill=1.0, base=0,
                                    pattern=[[-1, P]], channel_multiplier=1).then_inc(consts_ready, 1)
            nc.gpsimd.memset(bout_sb[:, :, :], 0.0).then_inc(bout_zeroed, 1)
            nc.gpsimd.memset(vbn[:, :, VB_Z:VB_K], 1.0).then_inc(vbn_set, 1)
            nc.gpsimd.memset(vbn[:, :, VB_K:P], 0.0).then_inc(vbn_set, 1)
            nc.gpsimd.memset(rep_f[:, :], 0.0).then_inc(rep_step, 1)
            for part in range(2):
                pool.wait_ge(rep_step, part + 1)
                nc.gpsimd.affine_select(out=rep_f[:, :], in_=rep_f[:, :], compare_op=ALU.not_equal, fill=1.0,
                                        base=-part * DM, pattern=[[0, H], [-1, DM]], channel_multiplier=1)\
                    .then_inc(rep_step, 1)
            pool.wait_ge(rep_step, 3)
            for b in range(B):
                nc.gpsimd.tensor_copy(rep[:, b, :], rep_f[:, :]).then_inc(rep_ready, 1)
            nc.gpsimd.memset(vblk[:, :, :], 0.0).then_inc(vblk_zeroed, 1)
            nc.gpsimd.memset(w[:, :, :], 0.0).then_inc(w_set, 1)
            pool.wait_ge(w_set, 1)
            nc.gpsimd.memset(w[:, :, Z_ROW + 1:Z_ROW + 2], 1.0).then_inc(w_set, 1)

            def split_lo(i, k):
                i2, s = slot_of(i, k)
                pool.wait_ge(xh_ready, TPG * i + k + 1)
                free(pool, self_done[s], i2)
                nc.gpsimd.tensor_tensor(xl[:, s, :, :], xT_sb[:, s, :, :], xh[:, s, :, :].bitcast(F32),
                                        ALU.subtract).then_inc(xl_ready, 1)

            split_lo(0, 0)
            split_lo(0, 1)

            def turn(i, last):
                for k in range(TPG):
                    if not (last and k >= TPG - 2):
                        split_lo(i, k + 2)

            turn(0, False)
            with pool.Fori(1, G - 1) as i:
                turn(i, False)
            turn(G - 1, True)

        return nc


def kernel(**inputs):
    import numpy as np
    import concourse.bacc as bacc
    from concourse.bass_utils import run_bass_kernel_spmd

    def arr(name):
        return np.asarray(inputs[name])

    x = arr("x")
    adj = arr("mask_BxSxSx11_ik0")
    pre = "L0_cond_"
    n = x.shape[1]
    groups = B * n // (P * TPG)
    x_t = x.reshape(groups, TPG, P, F)
    xT = x_t.reshape(groups, TPG, P, KC, P).transpose(0, 1, 4, 3, 2)
    a0 = adj[:, :, :NG, :].transpose(0, 1, 3, 2)
    a1 = adj[:, :NG, :, :].transpose(0, 2, 3, 1)
    a = np.concatenate([a0, a1], axis=3).reshape(groups, TPG, P, L, DM).transpose(0, 2, 1, 3, 4)

    def columns(v):
        return v.reshape(-1, P).T

    cols = np.concatenate([
        columns(arr(pre + "b_self")), columns(arr(pre + "bq")), columns(arr(pre + "bk")),
        arr("cond_1024").reshape(B, KC, P).transpose(2, 1, 0).reshape(P, KC * B),
        np.broadcast_to(arr(pre + "w_bias"), (P, L)), np.broadcast_to(arr(pre + "b_bias"), (P, 1))], axis=1)
    w_self = arr(pre + "W_self")
    arrays = {
        "x": x_t, "xT": xT, "x20": x[:, :NG].reshape(B * NG, F), "adj": a,
        "wselfT": w_self.T, "w1": w_self[:, :F],
        "wqT": arr(pre + "Wq").transpose(0, 2, 1), "wkT": arr(pre + "Wk").transpose(0, 2, 1),
        "woT": arr(pre + "Wout").reshape(ND, F, F).transpose(0, 2, 1),
        "cols": cols, "bout": arr(pre + "bout").reshape(1, ND, F),
    }
    arrays = {k: np.ascontiguousarray(v) for k, v in arrays.items()}

    nc = bacc.Bacc("TRN2", target_bir_lowering=False, num_devices=1)
    aps = {k: nc.dram_tensor(f"in_{k}", v.shape, mybir.dt.from_np(v.dtype), kind="ExternalInput").ap()
           for k, v in arrays.items()}
    out = nc.dram_tensor("out", x_t.shape, F32, kind="ExternalOutput").ap()
    build(nc, *(aps[k] for k in arrays), out)
    r = run_bass_kernel_spmd(nc, [{f"in_{k}": v for k, v in arrays.items()}], core_ids=[0])
    return r.results[0]["out"].reshape(B, n, F)
```

```python
from contextlib import ExitStack

import concourse.bass as bass
from concourse import mybir

F32 = mybir.dt.float32
F32R = mybir.dt.float32r
I32 = mybir.dt.int32
ALU = mybir.AluOpType
ACT = mybir.ActivationFunctionType
AX_X = mybir.AxisListType.X

P = 128
B = 2
F = 512
H = 16
DH = F // H
NG = 20
ND = 2
L = 11
DM = ND * NG
HM = H * DM
HALF = HM // 2
KC = F // P
TPG = 4
HPG = 3
NB = (H + HPG - 1) // HPG
BK = HPG * DM
BF = HPG * DH
Z_ROW = BK
VB_Z = 2 * DM
VB_K = VB_Z + 4
NEG = -9000000000000000.0
HUGE = 3.0e38
SCALE = float(DH) ** -0.5

C_BSELF = 0
C_BQ = C_BSELF + KC
C_BK = C_BQ + ND * KC
C_Q = C_BK + ND * KC
C_WB = C_Q + KC * B
C_BB = C_WB + L
NCOLS = C_BB + 1


def build(nc, x, xT, x20, adj, wselfT, w1, wqT, wkT, woT, cols, bout, out):
    G = x.shape[0]
    GPB = G // B
    N20 = B * NG

    with ExitStack() as ctx:
        def sb(name, shape, dt=F32):
            return ctx.enter_context(nc.sbuf_tensor(name, shape, dt))

        def sem(name):
            return ctx.enter_context(nc.semaphore(name))

        def sems(name, n):
            return [sem(f"{name}{j}") for j in range(n)]

        ws_hi = sb("ws_hi", [P, KC, F], F32R)
        ws_lo = sb("ws_lo", [P, KC, F], F32R)
        w2_hi = sb("w2_hi", [P, KC, F], F32R)
        w2_lo = sb("w2_lo", [P, KC, F], F32R)
        w1_hi = sb("w1_hi", [P, KC, F], F32R)
        w1_lo = sb("w1_lo", [P, KC, F], F32R)
        wq_hi = sb("wq_hi", [P, KC, F], F32R)
        wq_lo = sb("wq_lo", [P, KC, F], F32R)
        g_hi = sb("g_hi", [P, B, KC, HM], F32R)
        g_lo = sb("g_lo", [P, B, KC, HM], F32R)
        cols_sb = sb("cols_sb", [P, NCOLS])
        ident = sb("ident", [P, P])
        ones = sb("ones", [P, P])
        x20_sb = sb("x20_sb", [N20, F])
        vcq = sb("vcq", [P, 2 * KC, N20 + B])
        vcq_hi = sb("vcq_hi", [P, 2 * KC, N20 + B], F32R)
        vcq_lo = sb("vcq_lo", [P, 2 * KC, N20 + B], F32R)
        rows_a = sb("rows_a", [N20 + B, ND, F])
        rows_q = sb("rows_q", [B + 1, ND, F])
        crow = sb("crow", [B + 1, F])
        z20 = sb("z20", [P, N20])
        s20T = sb("s20T", [P, KC, N20 + B + 1])
        s20T_hi = sb("s20T_hi", [P, KC, N20 + B + 1], F32R)
        s20T_lo = sb("s20T_lo", [P, KC, N20 + B + 1], F32R)
        keyblk = sb("keyblk", [P, ND * KC, B, 4, NG])
        qc = sb("qc", [P, ND * KC, B + 1])
        rep = sb("rep", [P, B, HM], F32R)
        vblk = sb("vblk", [P, B, F])
        bout_sb = sb("bout_sb", [B + 1, ND, F])
        m_sb = sb("m_sb", [P, ND * KC, F])
        def as_wk(t):
            return t[:, :, :, :].rearrange("p a b c -> p (a b c)")[:, 0:ND * KC * F]\
                .rearrange("p (d c n) -> p d c n", d=ND, c=KC)

        gc_hi, gc_lo = (t[0:B + 1, :, :].rearrange("p a b -> p (a b)")[:, 0:B * HM]
                        .rearrange("p (b n) -> p b n", b=B) for t in (wq_hi, wq_lo))
        wk_hi, wk_lo = as_wk(g_hi), as_wk(g_lo)
        wo_hi, wo_lo = (w2_hi, w1_hi), (w2_lo, w1_lo)
        m_flat = m_sb[:, :, :].rearrange("p a b -> p (a b)")
        rep_f = m_flat[:, (ND * KC - 2) * F:(ND * KC - 2) * F + HM]
        logit = m_flat[:, 0:HM]
        expd = m_flat[:, HM:2 * HM]
        wT = m_flat[:, 2 * HM:2 * HM + NB * P]
        outb = m_flat[:, 2 * HM + NB * P:2 * HM + NB * P + 2 * F].rearrange("p (s n) -> p s n", s=2)

        xT_sb = sb("xT_sb", [P, TPG, KC, P])
        xh = sb("xh", [P, TPG, KC, P], F32R)
        xl = sb("xl", [P, TPG, KC, P], F32R)
        x_sb = sb("x_sb", [P, TPG, F])
        rowsum = sb("rowsum", [P, TPG])
        rs_junk = sb("rs_junk", [P, F])
        adj_sb = sb("adj_sb", [P, TPG, L, DM], I32)
        vb = sb("vb", [P, TPG, DM])
        cond = sb("cond", [P, TPG, DM])
        negvb = sb("negvb", [P, TPG, DM])
        cap = sb("cap", [P, TPG, DM])
        vbn = sb("vbn", [P, TPG, P])
        vbT = sb("vbT", [P, 2, P], F32R)
        mx = sb("mx", [P, H * ND])
        den = sb("den", [P, H * ND])
        rden = sb("rden", [P, H * ND])
        w = sb("w", [P, NB, P])

        def ps(name, shape):
            return ctx.enter_context(nc.psum_tensor(name, shape, F32))

        lgP = ps("lgP", [P, 2, 512])
        outP = [ps("outP0", [P, 512]), ps("outP1", [P, 512])]
        trP = ps("trP", [P, 2, 512])
        auxP = [ps("auxP0", [P, 512]), ps("auxP1", [P, 512])]
        foldP = [lgP[:, 0, :], lgP[:, 1, :], outP[0][:, :], outP[1][:, :]]

        x20_in, cols_in, bout_in = sem("x20_in"), sem("cols_in"), sem("bout_in")
        raw_in, part_hi, part_lo = sems("raw_in", 4), sem("part_hi"), sem("part_lo")
        consts_ready, keyblk_zeroed, bout_zeroed = sem("consts_ready"), sem("keyblk_zeroed"), sem("bout_zeroed")
        vbn_set, w_set, vblk_zeroed = sem("vbn_set"), sem("w_set"), sem("vblk_zeroed")
        x20T_done, vcqx_ready, sum20_done, z20_ready, vcq_ready = (
            sem("x20T_done"), sem("vcqx_ready"), sem("sum20_done"), sem("z20_ready"), sem("vcq_ready"))
        s20_done, s20_ready = sem("s20_done"), sem("s20_ready")
        rows_ready, s20T_done, s20T_set, qrow_done, qrow_ready, krow_done, krow_ready = (
            sem("rows_ready"), sem("s20T_done"), sem("s20T_set"), sem("qrow_done"), sem("qrow_ready"),
            sem("krow_done"), sem("krow_ready"))
        m_done, m_ready = sem("m_done"), sem("m_ready")
        k_done, key_ready, qc_done, qc_ready = sem("k_done"), sem("key_ready"), sem("qc_done"), sem("qc_ready")
        fold_done, fold_hi, fold_lo = sem("fold_done"), sem("fold_hi"), sem("fold_lo")
        v_done, v_ready, crow_done, crow_ready = sem("v_done"), sem("v_ready"), sem("crow_done"), sem("crow_ready")
        vblk_in, rep_in, rep_ready, rep_step = sem("vblk_in"), sem("rep_in"), sem("rep_ready"), sem("rep_step")
        vb01_done, vb01_ready, vbT_ready = sem("vb01_done"), sem("vb01_ready"), sem("vbT_ready")
        vbtr_done = sem("vbtr_done")

        xT_in, x_in = sems("xT_in", TPG), sems("x_in", TPG)
        adj_in, adj_used = sem("adj_in"), sem("adj_used")
        xh_ready, xl_ready, rowsum_ready, z_ready = sem("xh_ready"), sem("xl_ready"), sem("rowsum_ready"), sem("z_ready")
        vb_step, vb_ready, cap_ready = sem("vb_step"), sem("vb_ready"), sem("cap_ready")
        lg_done, self_done = sem("lg_done"), sems("self_done", TPG)
        masked, max_ready, shifted, exp_ready = sem("masked"), sem("max_ready"), sem("shifted"), sem("exp_ready")
        den_ready, rden_ready, w_ready = sem("den_ready"), sem("rden_ready"), sem("w_ready")
        tr_done, tr_copied = sem("tr_done"), sem("tr_copied")
        pv_done, fin_ready, stored = sem("pv_done"), sem("fin_ready"), sems("stored", 2)

        W_STEPS = 3
        TR_COPIES = 2
        VB_STEPS = L + 3
        LABELS = (0, 2, 7, 9, L)

        def raw(n):
            t = xT_sb[:, :, :, :].rearrange("p a b c -> p (a b c)") if n % 4 < 2 else \
                x_sb[:, :, :].rearrange("p a b -> p (a b)")
            return t[:, (n % 2) * 2 * F:(n % 2 + 1) * 2 * F].rearrange("p (c n) -> p c n", c=2)

        def halves(dram, hi, lo):
            return [(dram[a * P:(a + 2) * P, :].rearrange("(c p) n -> p c n", p=P), hi[:, a:a + 2, :], lo[:, a:a + 2, :])
                    for a in range(0, KC, 2)]

        pieces = halves(wselfT[0:F], ws_hi, ws_lo) + halves(wselfT[F:2 * F], w2_hi, w2_lo)
        WS_PARTS = len(pieces)
        pieces += halves(w1, w1_hi, w1_lo) + halves(wqT[0], wq_hi, wq_lo)
        WQ0_PARTS = len(pieces)
        pieces += halves(wkT[0], wk_hi[:, 0], wk_lo[:, 0]) + halves(wkT[1], wk_hi[:, 1], wk_lo[:, 1])
        WK_PARTS = len(pieces)
        pieces += halves(woT[0], wo_hi[0], wo_lo[0])
        WO0_PARTS = len(pieces)
        pieces += halves(wqT[1], wq_hi, wq_lo)
        WQ1_PARTS = len(pieces)
        pieces += halves(woT[1], wo_hi[1], wo_lo[1])

        def slot_of(i, k):
            return i + k // TPG, k % TPG

        def free(eng, s, n):
            if not (isinstance(n, int) and n <= 0):
                eng.wait_ge(s, n)

        block = ctx.enter_context(nc.Block())

        @block.sync
        def _(sp):
            sp.dma_start(x20_sb[:, :], x20).then_inc(x20_in, 16)
            sp.dma_start(cols_sb[:, :], cols).then_inc(cols_in, 16)
            for n, (src, _, _) in enumerate(pieces):
                if n >= 4:
                    sp.wait_ge(part_lo, n - 3)
                sp.dma_start(raw(n), src).then_inc(raw_in[n % 4], 16)
                if n == WQ0_PARTS:
                    sp.dma_start(adj_sb[:, :, :, :], adj[0]).then_inc(adj_in, 16)
                if n == WK_PARTS:
                    sp.wait_ge(bout_zeroed, 1)
                    sp.dma_start(bout_sb[B:B + 1, :, :], bout).then_inc(bout_in, 16)
            sp.wait_ge(part_lo, len(pieces))
            for k in range(TPG):
                sp.dma_start(xT_sb[:, k, :, :], xT[0, k]).then_inc(xT_in[k], 16)
                sp.dma_start(x_sb[:, k, :], x[0, k]).then_inc(x_in[k], 16)
            sp.wait_ge(vblk_zeroed, 1)
            sp.wait_ge(crow_ready, 2)
            for b in range(B):
                sp.dma_start(vblk[Z_ROW:Z_ROW + 1, b, :], crow[b:b + 1, :]).then_inc(vblk_in, 16)
                sp.dma_start(vblk[Z_ROW + 1:Z_ROW + 2, b, :], crow[B:B + 1, :]).then_inc(vblk_in, 16)

            def value_rows(d):
                sp.wait_ge(v_ready, d + 1)
                for b in range(B):
                    for j in range(HPG):
                        r = slice(j * DM + d * NG, j * DM + (d + 1) * NG)
                        sp.dma_start(vblk[r, b, :].rearrange("p (h n) -> p h n", n=DH)[:, j::HPG, :],
                                     rows_a[b * NG:(b + 1) * NG, d, :].rearrange("p (h n) -> p h n", n=DH)[:, j::HPG, :])\
                            .then_inc(vblk_in, 16)

            value_rows(0)
            sp.wait_ge(fold_hi, KC * (KC + 1))
            sp.wait_ge(fold_lo, KC * (KC + 1))
            sp.wait_ge(rep_ready, 2)
            for r, part in enumerate((gc_hi, gc_lo)):
                for b in range(B):
                    sp.dma_start(rep[VB_Z + r:VB_Z + r + 1, b, :].bitcast(F32), part[b:b + 1, b, :].bitcast(F32)).then_inc(rep_in, 16)
                sp.dma_start(rep[VB_Z + 2 + r:VB_Z + 3 + r, :, :].bitcast(F32), part[B:B + 1, :, :].bitcast(F32)).then_inc(rep_in, 16)
            value_rows(1)

            sp.wait_ge(adj_used, 1)
            sp.dma_start(adj_sb[:, :, :, :], adj[1]).then_inc(adj_in, 16)

            def turn(i, more, more_adj):
                for k in range(TPG):
                    if more:
                        sp.wait_ge(xl_ready, TPG * i + k + 1)
                        sp.dma_start(xT_sb[:, k, :, :], xT[i + 1, k]).then_inc(xT_in[k], 16)
                    sp.wait_ge(fin_ready, TPG * i + k + 1)
                    sp.dma_start(out[i, k], outb[:, k % 2, :]).then_inc(stored[k % 2], 16)
                    if more:
                        sp.dma_start(x_sb[:, k, :], x[i + 1, k]).then_inc(x_in[k], 16)
                    if more_adj and k == TPG - 2:
                        sp.wait_ge(adj_used, i + 2)
                        sp.dma_start(adj_sb[:, :, :, :], adj[i + 2]).then_inc(adj_in, 16)

            turn(0, True, True)
            with sp.Fori(1, G - 2) as i:
                turn(i, True, True)
            turn(G - 2, True, False)
            turn(G - 1, False, False)
            for s in range(2):
                sp.wait_ge(stored[s], 16 * G * TPG // 2)

        @block.tensor
        def _(pe):
            def mm(o, a, b, start, stop):
                return nc.tensor.matmul(o, a, b, start=start, stop=stop, skip_group_check=True)

            pe.wait_ge(x20_in, 16)
            pe.wait_ge(consts_ready, 3)
            for c in range(KC):
                last = nc.tensor.transpose(auxP[0][:, c * N20:(c + 1) * N20], x20_sb[:, c * P:(c + 1) * P],
                                           ident[0:N20, 0:N20])
            last.then_inc(x20T_done, 1)
            pe.wait_ge(vcqx_ready, 2)
            for c in range(KC):
                last = mm(auxP[1][:, 0:N20], ones[:, :], vcq[:, c, 0:N20], c == 0, c == KC - 1)
            last.then_inc(sum20_done, 1)

            def passes(o, pairs):
                for n, (a_hi, a_lo, b_hi, b_lo) in enumerate(pairs):
                    mm(o, a_hi, b_hi, n == 0, False)
                    mm(o, a_hi, b_lo, False, False)
                    last = mm(o, a_lo, b_hi, False, n == len(pairs) - 1)
                return last

            pe.wait_ge(vcq_ready, 4)
            pe.wait_ge(part_lo, WS_PARTS)
            passes(trP[0:N20 + B, 0, :], [(vcq_hi[:, c, :], vcq_lo[:, c, :], h[:, c % KC, :], lo[:, c % KC, :])
                                          for c in range(2 * KC)
                                          for h, lo in (((ws_hi, ws_lo), (w2_hi, w2_lo))[c // KC],)])\
                .then_inc(s20_done, 1)

            def fold_w(d, c):
                n = d * KC + c
                if n >= 4:
                    pe.wait_ge(m_ready, n - 3)
                cs = slice(c * P, (c + 1) * P)
                passes(foldP[n % 4], [(wq_hi[:, f, cs], wq_lo[:, f, cs], w1_hi[:, f, :], w1_lo[:, f, :])
                                      for f in range(KC)]).then_inc(m_done, 1)

            def q_rows(d):
                if d:
                    pe.wait_ge(qrow_ready, d)
                cc = slice(N20, N20 + B + 1)
                passes(auxP[1][0:B + 1, :], [(s20T_hi[:, f, cc], s20T_lo[:, f, cc], wq_hi[:, f, :], wq_lo[:, f, :])
                                             for f in range(KC)]).then_inc(qrow_done, 1)

            def v_rows(d):
                passes(trP[0:N20, 1 - d, :], [(s20T_hi[:, f, 0:N20], s20T_lo[:, f, 0:N20],
                                               wo_hi[d][:, f, :], wo_lo[d][:, f, :]) for f in range(KC)])\
                    .then_inc(v_done, 1)

            pe.wait_ge(part_lo, WQ0_PARTS)
            fold_w(0, 0)
            pe.wait_ge(rows_ready, 1)
            for f in range(KC):
                last = nc.tensor.transpose(auxP[0][:, f * 64:f * 64 + N20 + B],
                                           rows_a[0:N20 + B, 0, f * P:(f + 1) * P], ident[0:N20 + B, 0:N20 + B])
            last.then_inc(s20T_done, 1)
            for c in range(1, KC):
                fold_w(0, c)
            pe.wait_ge(s20_ready, 3)
            pe.wait_ge(s20T_set, 2)
            q_rows(0)
            pe.wait_ge(part_lo, WK_PARTS)
            for d in range(ND):
                passes(trP[0:N20, d, :], [(s20T_hi[:, f, 0:N20], s20T_lo[:, f, 0:N20],
                                           wk_hi[:, d, f, :], wk_lo[:, d, f, :]) for f in range(KC)])\
                    .then_inc(krow_done, 1)
            pe.wait_ge(part_lo, WQ1_PARTS)
            fold_w(1, 0)
            pe.wait_ge(krow_ready, ND)
            for n in range(ND * KC):
                last = nc.tensor.transpose(auxP[0][:, n * N20:(n + 1) * N20],
                                           rows_a[0:N20, n // KC, n % KC * P:(n % KC + 1) * P], ident[0:N20, 0:N20])
            last.then_inc(k_done, 1)
            for c in range(1, KC):
                fold_w(1, c)
            q_rows(1)
            pe.wait_ge(key_ready, 4)
            for f in range(KC):
                last = nc.tensor.transpose(auxP[0][0:B + 1, f * P:(f + 1) * P], s20T[:, f, N20:N20 + B + 1], ident[:, :])
            last.then_inc(crow_done, 1)
            v_rows(0)
            pe.wait_ge(qrow_ready, ND)
            for n in range(ND * KC):
                last = nc.tensor.transpose(trP[:, 0, n * 4:n * 4 + B + 1],
                                           rows_q[:, n // KC, n % KC * P:(n % KC + 1) * P], ident[0:B + 1, 0:B + 1])
            last.then_inc(qc_done, 1)
            pe.wait_ge(m_ready, ND * KC)
            pe.wait_ge(key_ready, 4)
            pe.wait_ge(qc_ready, 2)
            n = 0
            for c in range(KC):
                for ic in range(KC + 1):
                    if n >= 4:
                        pe.wait_ge(fold_hi, n - 3)
                        pe.wait_ge(fold_lo, n - 3)
                    for d in range(ND):
                        if ic < KC:
                            o, a = foldP[n % 4], m_sb[:, d * KC + c, ic * P:(ic + 1) * P]
                        else:
                            o, a = foldP[n % 4][0:B + 1], qc[:, d * KC + c, :]
                        o = o[:, 0:B * 4 * DM].rearrange("p (b h n) -> p b h n", b=B, h=4)[:, :, :, d * NG:(d + 1) * NG]
                        last = mm(o, a, keyblk[:, d * KC + c, :, :, :], d == 0, d == 1)
                    last.then_inc(fold_done, 1)
                    n += 1
            pe.wait_ge(part_lo, len(pieces))
            v_rows(1)
            pe.wait_ge(vb_ready, 1)
            pe.wait_ge(z_ready, 2)
            for k in range(2):
                last = nc.tensor.transpose(auxP[1][:, k * P:(k + 1) * P], vbn[:, k, :], ident[:, :])
            last.then_inc(vb01_done, 1)

            def logits(i, k, b, first=False):
                t = TPG * i + k
                pe.wait_ge(xh_ready, t + 1)
                pe.wait_ge(xl_ready, t + 1)
                free(pe, masked, t)
                s = k % TPG
                for c in range(KC):
                    for a, g in ((xh, g_hi), (xh, g_lo), (xl, g_hi)):
                        for h in range(2):
                            mm(lgP[:, h, 0:HALF], a[:, s, c, :], g[:, b, c, h * HALF:(h + 1) * HALF],
                               c == 0 and a is xh and g is g_hi, False)
                if not first:
                    free(pe, vbT_ready, t - 1)
                for h in range(2):
                    last = mm(lgP[:, h, 0:HALF], vbT[0:VB_K, k % 2, :], rep[0:VB_K, b, h * HALF:(h + 1) * HALF],
                              False, True)
                last.then_inc(lg_done, 1)

            def self_rows(i, k, first=False):
                t = TPG * i + k
                if not first:
                    free(pe, fin_ready, t - 1)
                s = k % TPG
                for c in range(KC):
                    for a, g in ((xh, ws_hi), (xh, ws_lo), (xl, ws_hi)):
                        last = mm(outP[k % 2][:, :], a[:, s, c, :], g[:, c, :],
                                  c == 0 and a is xh and g is ws_hi, False)
                last.then_inc(self_done[s], 1)

            def turned(i, k):
                t = TPG * i + k
                pe.wait_ge(w_ready, W_STEPS * t + W_STEPS)
                free(pe, tr_copied, TR_COPIES * t)
                for e in range(NB):
                    last = nc.tensor.transpose(trP[:, e // 4, (e % 4) * P:(e % 4 + 1) * P], w[:, e, :], ident[:, :])
                last.then_inc(tr_done, 1)

            def turned_vb(i, k):
                t = TPG * i + k
                i2, s2 = slot_of(i, k)
                free(pe, vbT_ready, t - 2)
                pe.wait_ge(vb_ready, i2 + 1)
                pe.wait_ge(z_ready, t + 1)
                nc.tensor.transpose(auxP[0][:, 0:P], vbn[:, s2, :], ident[:, :]).then_inc(vbtr_done, 1)

            def values(i, k, b):
                t = TPG * i + k
                pe.wait_ge(tr_copied, TR_COPIES * t + TR_COPIES)
                for e in range(NB):
                    n = min(BF, F - e * BF)
                    last = mm(outP[k % 2][:, e * BF:e * BF + n], wT[:, e * P:(e + 1) * P],
                              vblk[:, b, e * BF:e * BF + n], False, e == NB - 1)
                last.then_inc(pv_done, 1)

            pe.wait_ge(fold_hi, KC * (KC + 1))
            pe.wait_ge(fold_lo, KC * (KC + 1))
            pe.wait_ge(rep_in, 16 * 2 * (B + 1))
            pe.wait_ge(vb01_ready, 1)
            pe.wait_ge(v_ready, ND)
            logits(0, 0, 0, first=True)
            self_rows(0, 0, first=True)
            pe.wait_ge(vblk_in, 16 * (B * ND * HPG + 2 * B))

            def turn(i, last):
                b = i // GPB
                for k in range(TPG):
                    more = not (last and k == TPG - 1)
                    if more:
                        i1, _ = slot_of(i, k + 1)
                        logits_next = (i, k + 1) if k + 1 < TPG else (i + 1, 0)
                        logits(*logits_next, logits_next[0] // GPB)
                    turned(i, k)
                    if not (last and k >= TPG - 2):
                        turned_vb(i, k + 2)
                    if more:
                        self_rows(*logits_next)
                    values(i, k, b)

            turn(0, False)
            with pe.Fori(1, G - 1) as i:
                turn(i, False)
            turn(G - 1, True)

        @block.scalar
        def _(act):
            def split_hi(i, k):
                i2, s = slot_of(i, k)
                act.wait_ge(xT_in[s], 16 * i2 + 16)
                free(act, self_done[s], i2)
                nc.scalar.activation(xh[:, s, :, :], xT_sb[:, s, :, :], ACT.Copy).then_inc(xh_ready, 1)
                act.wait_ge(x_in[s], 16 * i2 + 16)
                free(act, rowsum_ready, TPG * i + k)
                nc.scalar.activation(rs_junk[:, :], x_sb[:, s, :], ACT.Copy,
                                     accum_out=rowsum[:, s:s + 1]).then_inc(rowsum_ready, 1)

            def upper(first, end):
                for n in range(first, end):
                    act.wait_ge(raw_in[n % 4], 16 * (n // 4) + 16)
                    nc.scalar.activation(pieces[n][1], raw(n), ACT.Copy).then_inc(part_hi, 1)

            def copy_m(n):
                act.wait_ge(m_done, n + 1)
                nc.scalar.activation(m_sb[:, n, :], foldP[n % 4], ACT.Copy).then_inc(m_ready, 1)

            def copy_q(d):
                act.wait_ge(qrow_done, d + 1)
                nc.scalar.activation(rows_q[:, d, :], auxP[1][0:B + 1, :], ACT.Copy).then_inc(qrow_ready, 1)

            upper(0, WQ0_PARTS)
            act.wait_ge(s20_done, 1)
            nc.scalar.activation(rows_a[:, 0, :], trP[0:N20 + B, 0, :], ACT.Copy).then_inc(rows_ready, 1)
            copy_m(0)
            upper(WQ0_PARTS, WQ0_PARTS + 2)
            copy_m(1)
            upper(WQ0_PARTS + 2, WK_PARTS)
            copy_m(2)
            upper(WK_PARTS, WO0_PARTS)
            copy_m(3)
            copy_q(0)
            upper(WO0_PARTS, WQ1_PARTS)
            act.wait_ge(s20T_done, 1)
            for d in range(ND):
                act.wait_ge(krow_done, d + 1)
                nc.scalar.activation(rows_a[0:N20, d, :], trP[0:N20, d, :], ACT.Copy).then_inc(krow_ready, 1)
            act.wait_ge(rep_ready, 2)
            for n in range(KC, ND * KC):
                copy_m(n)
            upper(WQ1_PARTS, len(pieces))
            copy_q(1)
            act.wait_ge(k_done, 1)
            act.wait_ge(v_done, 1)
            nc.scalar.activation(rows_a[0:N20, 0, :], trP[0:N20, 1, :], ACT.Copy).then_inc(v_ready, 1)
            split_hi(0, 0)
            split_hi(0, 1)
            split_hi(0, 2)
            n = 0
            for c in range(KC):
                for ic in range(KC + 1):
                    act.wait_ge(fold_done, n + 1)
                    if ic < KC:
                        o, a = g_hi[:, :, ic, :], foldP[n % 4]
                    else:
                        o, a = gc_hi, foldP[n % 4][0:B + 1]
                    nc.scalar.activation(o[:, :, c * 4 * DM:(c + 1) * 4 * DM].bitcast(F32R),
                                         a[:, 0:B * 4 * DM].rearrange("p (b n) -> p b n", b=B),
                                         ACT.Copy, scale=SCALE).then_inc(fold_hi, 1)
                    n += 1
            act.wait_ge(v_done, 2)
            nc.scalar.activation(rows_a[0:N20, 1, :], trP[0:N20, 0, :], ACT.Copy).then_inc(v_ready, 1)
            act.wait_ge(vb01_done, 1)
            nc.scalar.activation(vbT[:, :, :], auxP[1][:, 0:2 * P].rearrange("p (s n) -> p s n", s=2), ACT.Copy)\
                .then_inc(vb01_ready, 1)

            def exponentials(i, k):
                t = TPG * i + k
                act.wait_ge(shifted, t + 1)
                free(act, w_ready, W_STEPS * t)
                nc.scalar.activation(expd, logit, ACT.Exp).then_inc(exp_ready, 1)

            exponentials(0, 0)

            def turn(i, last):
                for k in range(TPG):
                    t = TPG * i + k
                    act.wait_ge(tr_done, t + 1)
                    free(act, pv_done, t)
                    nc.scalar.activation(wT[:, 0:4 * P], trP[:, 0, :], ACT.Copy).then_inc(tr_copied, 1)
                    nc.scalar.activation(wT[:, 4 * P:NB * P], trP[:, 1, 0:2 * P], ACT.Copy).then_inc(tr_copied, 1)
                    if not (last and k >= TPG - 2):
                        act.wait_ge(vbtr_done, t + 1)
                        act.wait_ge(lg_done, t + 1)
                        nc.scalar.activation(vbT[:, k % 2, :], auxP[0][:, 0:P], ACT.Copy).then_inc(vbT_ready, 1)
                    if not (last and k >= TPG - 1):
                        exponentials(*((i, k + 1) if k + 1 < TPG else (i + 1, 0)))
                    if not (last and k >= TPG - 3):
                        split_hi(i, k + 3)

            turn(0, False)
            with act.Fori(1, G - 1) as i:
                turn(i, False)
            turn(G - 1, True)

        @block.vector
        def _(dve):
            nc.vector.memset(vcq[:, 0:KC, N20:N20 + B], 0.0).then_inc(vcqx_ready, 1)
            nc.vector.memset(keyblk[:, :, :, :, :], 0.0).then_inc(keyblk_zeroed, 1)
            dve.wait_ge(x20T_done, 1)
            nc.vector.tensor_copy(vcq[:, 0:KC, 0:N20], auxP[0][:, 0:KC * N20].rearrange("p (c n) -> p c n", c=KC))\
                .then_inc(vcqx_ready, 1)
            dve.wait_ge(sum20_done, 1)
            nc.vector.tensor_scalar(z20[:, :], auxP[1][:, 0:N20], 0.0, None, ALU.not_equal).then_inc(z20_ready, 1)
            dve.wait_ge(cols_in, 16)
            q_cols = cols_sb[:, C_Q:C_Q + KC * B].rearrange("p (c b) -> p c b", b=B)
            dve.wait_ge(z20_ready, 1)
            nc.vector.tensor_tensor(
                vcq[:, KC:2 * KC, 0:N20].rearrange("p c (b m) -> p c b m", b=B),
                z20[:, :].rearrange("p (b m) -> p b m", b=B).unsqueeze(1).to_broadcast([P, KC, B, NG]),
                q_cols.unsqueeze(3).to_broadcast([P, KC, B, NG]), ALU.mult).then_inc(vcq_ready, 1)
            nc.vector.tensor_copy(vcq[:, KC:2 * KC, N20:N20 + B], q_cols).then_inc(vcq_ready, 1)
            dve.wait_ge(vcq_ready, 2)
            nc.vector.tensor_copy(vcq_hi[:, :, :], vcq[:, :, :]).then_inc(vcq_ready, 1)
            dve.wait_ge(vcq_ready, 3)
            nc.vector.tensor_tensor(vcq_lo[:, :, :], vcq[:, :, :], vcq_hi[:, :, :].bitcast(F32), ALU.subtract)\
                .then_inc(vcq_ready, 1)

            def lower(first, end):
                for n in range(first, end):
                    dve.wait_ge(part_hi, n + 1)
                    nc.vector.tensor_tensor(pieces[n][2], raw(n), pieces[n][1].bitcast(F32), ALU.subtract)\
                        .then_inc(part_lo, 1)

            lower(0, WQ0_PARTS)
            b_self = cols_sb[:, C_BSELF:C_BSELF + KC]
            dve.wait_ge(s20T_done, 1)
            s20P = auxP[0][:, 0:KC * 64].rearrange("p (c n) -> p c n", c=KC)
            nc.vector.tensor_tensor(s20T[:, :, 0:N20], s20P[:, :, 0:N20],
                                    b_self.unsqueeze(2).to_broadcast([P, KC, N20]), ALU.add).then_inc(s20_ready, 1)
            nc.vector.tensor_copy(s20T[:, :, N20:N20 + B], s20P[:, :, N20:N20 + B]).then_inc(s20_ready, 1)
            nc.vector.tensor_copy(s20T[:, :, N20 + B:N20 + B + 1], b_self.unsqueeze(2)).then_inc(s20_ready, 1)
            dve.wait_ge(s20_ready, 3)
            nc.vector.tensor_copy(s20T_hi[:, :, :], s20T[:, :, :]).then_inc(s20T_set, 1)
            dve.wait_ge(s20T_set, 1)
            nc.vector.tensor_tensor(s20T_lo[:, :, :], s20T[:, :, :], s20T_hi[:, :, :].bitcast(F32), ALU.subtract)\
                .then_inc(s20T_set, 1)
            lower(WQ0_PARTS, WQ1_PARTS)

            adj_l = [adj_sb[:, :, j, :] for j in range(L)]
            w_bias = [cols_sb[:, C_WB + j:C_WB + j + 1] for j in range(L)]

            def link(ins, i, step):
                ins.then_inc(vb_step, 1)
                dve.wait_ge(vb_step, VB_STEPS * i + step)

            def edge_bias(i, first, end):
                if first == 0:
                    dve.wait_ge(adj_in, 16 * i + 16)
                    link(nc.vector.tensor_scalar(vb[:, :, :], adj_l[0], w_bias[0], cols_sb[:, C_BB:C_BB + 1],
                                                 ALU.mult, ALU.add), i, 1)
                for j in range(max(first, 1), end):
                    link(nc.vector.scalar_tensor_tensor(vb[:, :, :], adj_l[j], w_bias[j], vb[:, :, :],
                                                        ALU.mult, ALU.add), i, j + 1)

            def edge_rows(i):
                link(nc.vector.tensor_copy(vbn[:, :, 0:DM].bitcast(F32R), vb[:, :, :]), i, L + 1)
                nc.vector.tensor_tensor(vbn[:, :, DM:2 * DM].bitcast(F32R), vb[:, :, :], vbn[:, :, 0:DM],
                                        ALU.subtract).then_inc(vb_ready, 1)

            def edge_cap(i):
                ins = nc.vector.tensor_reduce(cond[:, :, :], adj_sb[:, :, :, :].rearrange("p t l m -> p t m l"),
                                              AX_X, ALU.add)
                link(ins, i, L + 2)
                nc.vector.tensor_scalar(negvb[:, :, :], vb[:, :, :], NEG, None, ALU.add).then_inc(adj_used, 1)

            def edge_cap_in(i):
                link(nc.vector.tensor_scalar(cond[:, :, :], cond[:, :, :], 0.0, HUGE, ALU.is_gt, ALU.mult), i, L + 3)
                dve.wait_ge(adj_used, i + 1)
                nc.vector.tensor_tensor(cap[:, :, :], negvb[:, :, :], cond[:, :, :], ALU.add).then_inc(cap_ready, 1)

            def row_flags(i, k):
                i2, s = slot_of(i, k)
                dve.wait_ge(rowsum_ready, TPG * i + k + 1)
                nc.vector.tensor_scalar(vbn[:, s, VB_Z:VB_Z + 2], rowsum[:, s:s + 1].to_broadcast([P, 2]),
                                        0.0, None, ALU.not_equal).then_inc(z_ready, 1)

            def shift(i, k):
                t = TPG * i + k
                dve.wait_ge(lg_done, t + 1)
                dve.wait_ge(cap_ready, i + 1)
                nc.vector.tensor_tensor(
                    logit.rearrange("p (a h n) -> p a h n", a=2, n=DM),
                    lgP[:, :, 0:HALF].rearrange("p a (h n) -> p a h n", n=DM),
                    cap[:, k, :].unsqueeze(1).unsqueeze(1).to_broadcast([P, 2, H // 2, DM]),
                    ALU.min).then_inc(masked, 1)
                dve.wait_ge(masked, t + 1)
                soft = logit.rearrange("p (g m) -> p g m", m=NG)
                nc.vector.tensor_reduce(mx[:, :], soft, AX_X, ALU.max).then_inc(max_ready, 1)
                dve.wait_ge(max_ready, t + 1)
                nc.vector.tensor_tensor(soft, soft, mx[:, :].unsqueeze(2).to_broadcast([P, H * ND, NG]),
                                        ALU.subtract).then_inc(shifted, 1)

            def weigh(i, k):
                t = TPG * i + k
                dve.wait_ge(exp_ready, t + 1)
                nc.vector.tensor_reduce(den[:, :], expd.rearrange("p (g m) -> p g m", m=NG), AX_X, ALU.add)\
                    .then_inc(den_ready, 1)
                dve.wait_ge(den_ready, t + 1)
                nc.vector.reciprocal(rden[:, :], den[:, :]).then_inc(rden_ready, 1)
                dve.wait_ge(rden_ready, t + 1)
                free(dve, tr_done, t)
                full = (NB - 1) * BK
                nf = full // NG
                nc.vector.tensor_tensor(
                    w[:, 0:NB - 1, 0:BK].rearrange("p e (g m) -> p e g m", m=NG),
                    expd[:, 0:full].rearrange("p (e g m) -> p e g m", e=NB - 1, m=NG),
                    rden[:, 0:nf].rearrange("p (e g) -> p e g", e=NB - 1).unsqueeze(3)
                    .to_broadcast([P, NB - 1, BK // NG, NG]), ALU.mult).then_inc(w_ready, 1)
                nc.vector.tensor_tensor(
                    w[:, NB - 1, 0:HM - full].rearrange("p (g m) -> p g m", m=NG),
                    expd[:, full:HM].rearrange("p (g m) -> p g m", m=NG),
                    rden[:, nf:].unsqueeze(2).to_broadcast([P, H * ND - nf, NG]), ALU.mult).then_inc(w_ready, 1)
                nc.vector.tensor_scalar(w[:, :, Z_ROW:Z_ROW + 1], rowsum[:, k:k + 1].unsqueeze(1)
                                        .to_broadcast([P, NB, 1]), 0.0, None, ALU.not_equal).then_inc(w_ready, 1)

            def finish(i, k):
                t = TPG * i + k
                dve.wait_ge(pv_done, t + 1)
                dve.wait_ge(x_in[k], 16 * i + 16)
                free(dve, stored[k % 2], 16 * (2 * i + k // 2))
                nc.vector.scalar_tensor_tensor(outb[:, k % 2, :], outP[k % 2][:, :], 0.0, x_sb[:, k, :],
                                               ALU.max, ALU.add).then_inc(fin_ready, 1)

            edge_bias(0, 0, L)
            dve.wait_ge(vbn_set, 2)
            edge_rows(0)
            edge_cap(0)
            edge_cap_in(0)
            b_k = cols_sb[:, C_BK:C_BK + ND * KC]
            kP = auxP[0][:, 0:ND * KC * N20].rearrange("p (c b m) -> p c b m", b=B, m=NG)
            dve.wait_ge(k_done, 1)
            dve.wait_ge(keyblk_zeroed, 1)
            for h in range(4):
                r = slice(h * DH, (h + 1) * DH)
                nc.vector.tensor_tensor(keyblk[r, :, :, h, :], kP[r],
                                        b_k[r].unsqueeze(2).unsqueeze(2).to_broadcast([DH, ND * KC, B, NG]),
                                        ALU.add).then_inc(key_ready, 1)
            lower(WQ1_PARTS, len(pieces))
            dve.wait_ge(crow_done, 1)
            dve.wait_ge(bout_in, 16)
            nc.vector.tensor_tensor(crow[:, :], auxP[0][0:B + 1, :], bout_sb[:, 0, :], ALU.add).then_inc(crow_ready, 1)
            dve.wait_ge(crow_ready, 1)
            nc.vector.tensor_tensor(crow[:, :], crow[:, :], bout_sb[:, 1, :], ALU.add).then_inc(crow_ready, 1)
            dve.wait_ge(qc_done, 1)
            qcP = trP[:, 0, 0:ND * KC * 4].rearrange("p (c n) -> p c n", n=4)
            nc.vector.tensor_copy(qc[:, :, 0:B], qcP[:, :, 0:B]).then_inc(qc_ready, 1)
            nc.vector.tensor_tensor(qc[:, :, B:B + 1], qcP[:, :, B:B + 1],
                                    cols_sb[:, C_BQ:C_BQ + ND * KC].unsqueeze(2), ALU.add).then_inc(qc_ready, 1)
            row_flags(0, 0)
            row_flags(0, 1)
            n = 0
            for c in range(KC):
                for ic in range(KC + 1):
                    dve.wait_ge(fold_hi, n + 1)
                    if ic < KC:
                        o, hi, a = g_lo[:, :, ic, :], g_hi[:, :, ic, :], foldP[n % 4]
                    else:
                        o, hi, a = gc_lo, gc_hi, foldP[n % 4][0:B + 1]
                    s = slice(c * 4 * DM, (c + 1) * 4 * DM)
                    nc.vector.scalar_tensor_tensor(o[:, :, s].bitcast(F32R),
                                                   a[:, 0:B * 4 * DM].rearrange("p (b n) -> p b n", b=B),
                                                   SCALE, hi[:, :, s].bitcast(F32), ALU.mult, ALU.subtract)\
                        .then_inc(fold_lo, 1)
                    n += 1
            shift(0, 0)
            dve.wait_ge(w_set, 2)
            weigh(0, 0)
            row_flags(0, 2)

            def turn(i, last):
                for k in range(TPG):
                    more = not (last and k == TPG - 1)
                    if more:
                        i1, k1 = (i, k + 1) if k + 1 < TPG else (i + 1, 0)
                        shift(i1, k1)
                    if not last and k < 2:
                        edge_bias(i + 1, LABELS[2 * k], LABELS[2 * k + 1])
                    if more:
                        weigh(i1, k1)
                    finish(i, k)
                    if not (last and k >= TPG - 3):
                        row_flags(i, k + 3)
                    if not last and k < 2:
                        edge_bias(i + 1, LABELS[2 * k + 1], LABELS[2 * k + 2])
                    if not last and k == 1:
                        dve.wait_ge(vbtr_done, TPG * i + 2)
                        edge_rows(i + 1)
                    if not last and k == 2:
                        edge_cap(i + 1)
                        edge_cap_in(i + 1)

            turn(0, False)
            with dve.Fori(1, G - 1) as i:
                turn(i, False)
            turn(G - 1, True)

        @block.gpsimd
        def _(pool):
            nc.gpsimd.memset(ident[:, :], 0.0).then_inc(consts_ready, 1)
            nc.gpsimd.memset(ones[:, :], 1.0).then_inc(consts_ready, 1)
            pool.wait_ge(consts_ready, 1)
            nc.gpsimd.affine_select(out=ident[:, :], in_=ident[:, :], compare_op=ALU.not_equal, fill=1.0, base=0,
                                    pattern=[[-1, P]], channel_multiplier=1).then_inc(consts_ready, 1)
            nc.gpsimd.memset(bout_sb[:, :, :], 0.0).then_inc(bout_zeroed, 1)
            nc.gpsimd.memset(vbn[:, :, VB_Z:VB_K], 1.0).then_inc(vbn_set, 1)
            nc.gpsimd.memset(vbn[:, :, VB_K:P], 0.0).then_inc(vbn_set, 1)
            nc.gpsimd.memset(rep_f, 0.0).then_inc(rep_step, 1)
            for part in range(2):
                pool.wait_ge(rep_step, part + 1)
                nc.gpsimd.affine_select(out=rep_f, in_=rep_f, compare_op=ALU.not_equal, fill=1.0,
                                        base=-part * DM, pattern=[[0, H], [-1, DM]], channel_multiplier=1)\
                    .then_inc(rep_step, 1)
            pool.wait_ge(rep_step, 3)
            for b in range(B):
                nc.gpsimd.tensor_copy(rep[:, b, :], rep_f).then_inc(rep_ready, 1)
            nc.gpsimd.memset(vblk[:, :, :], 0.0).then_inc(vblk_zeroed, 1)
            nc.gpsimd.memset(w[:, :, :], 0.0).then_inc(w_set, 1)
            pool.wait_ge(w_set, 1)
            nc.gpsimd.memset(w[:, :, Z_ROW + 1:Z_ROW + 2], 1.0).then_inc(w_set, 1)

            def split_lo(i, k):
                i2, s = slot_of(i, k)
                pool.wait_ge(xh_ready, TPG * i + k + 1)
                free(pool, self_done[s], i2)
                nc.gpsimd.tensor_tensor(xl[:, s, :, :], xT_sb[:, s, :, :], xh[:, s, :, :].bitcast(F32),
                                        ALU.subtract).then_inc(xl_ready, 1)

            split_lo(0, 0)
            split_lo(0, 1)
            split_lo(0, 2)

            def turn(i, last):
                for k in range(TPG):
                    if not (last and k >= TPG - 3):
                        split_lo(i, k + 3)

            turn(0, False)
            with pool.Fori(1, G - 1) as i:
                turn(i, False)
            turn(G - 1, True)

        return nc


def kernel(**inputs):
    import numpy as np
    import concourse.bacc as bacc
    from concourse.bass_utils import run_bass_kernel_spmd

    def arr(name):
        return np.asarray(inputs[name])

    x = arr("x")
    adj = arr("mask_BxSxSx11_ik0")
    pre = "L0_cond_"
    n = x.shape[1]
    groups = B * n // (P * TPG)
    x_t = x.reshape(groups, TPG, P, F)
    xT = x_t.reshape(groups, TPG, P, KC, P).transpose(0, 1, 4, 3, 2)
    a0 = adj[:, :, :NG, :].transpose(0, 1, 3, 2)
    a1 = adj[:, :NG, :, :].transpose(0, 2, 3, 1)
    a = np.concatenate([a0, a1], axis=3).reshape(groups, TPG, P, L, DM).transpose(0, 2, 1, 3, 4)

    def columns(v):
        return v.reshape(-1, P).T

    cols = np.concatenate([
        columns(arr(pre + "b_self")), columns(arr(pre + "bq")), columns(arr(pre + "bk")),
        arr("cond_1024").reshape(B, KC, P).transpose(2, 1, 0).reshape(P, KC * B),
        np.broadcast_to(arr(pre + "w_bias"), (P, L)), np.broadcast_to(arr(pre + "b_bias"), (P, 1))], axis=1)
    w_self = arr(pre + "W_self")
    arrays = {
        "x": x_t, "xT": xT, "x20": x[:, :NG].reshape(B * NG, F), "adj": a,
        "wselfT": w_self.T, "w1": w_self[:, :F],
        "wqT": arr(pre + "Wq").transpose(0, 2, 1), "wkT": arr(pre + "Wk").transpose(0, 2, 1),
        "woT": arr(pre + "Wout").reshape(ND, F, F).transpose(0, 2, 1),
        "cols": cols, "bout": arr(pre + "bout").reshape(1, ND, F),
    }
    arrays = {k: np.ascontiguousarray(v) for k, v in arrays.items()}

    nc = bacc.Bacc("TRN2", target_bir_lowering=False, num_devices=1)
    aps = {k: nc.dram_tensor(f"in_{k}", v.shape, mybir.dt.from_np(v.dtype), kind="ExternalInput").ap()
           for k, v in arrays.items()}
    out = nc.dram_tensor("out", x_t.shape, F32, kind="ExternalOutput").ap()
    build(nc, *(aps[k] for k in arrays), out)
    r = run_bass_kernel_spmd(nc, [{f"in_{k}": v for k, v in arrays.items()}], core_ids=[0])
    return r.results[0]["out"].reshape(B, n, F)
```

```python
from contextlib import ExitStack

import concourse.bass as bass
from concourse import mybir

F32 = mybir.dt.float32
F32R = mybir.dt.float32r
I32 = mybir.dt.int32
ALU = mybir.AluOpType
ACT = mybir.ActivationFunctionType
AX_X = mybir.AxisListType.X

P = 128
B = 2
F = 512
H = 16
DH = F // H
NG = 20
ND = 2
L = 11
DM = ND * NG
HM = H * DM
HALF = HM // 2
KC = F // P
TPG = 4
HPG = 3
NB = (H + HPG - 1) // HPG
BK = HPG * DM
BF = HPG * DH
Z_ROW = BK
VB_0 = DM
VB_Z = Z_ROW + 2
VB_K = VB_Z + 4
SLOTS = 2 * TPG
NEG = -9000000000000000.0
HUGE = 3.0e38
SCALE = float(DH) ** -0.5

C_BSELF = 0
C_BQ = C_BSELF + KC
C_BK = C_BQ + ND * KC
C_Q = C_BK + ND * KC
C_WB = C_Q + KC * B
C_BB = C_WB + L
NCOLS = C_BB + 1


def build(nc, x, xT, x20, adj, wselfT, w1, wqT, wkT, woT, cols, bout, out):
    G = x.shape[0]
    GPB = G // B
    N20 = B * NG

    with ExitStack() as ctx:
        def sb(name, shape, dt=F32):
            return ctx.enter_context(nc.sbuf_tensor(name, shape, dt))

        def sem(name):
            return ctx.enter_context(nc.semaphore(name))

        def sems(name, n):
            return [sem(f"{name}{j}") for j in range(n)]

        ws_hi = sb("ws_hi", [P, KC, F], F32R)
        ws_lo = sb("ws_lo", [P, KC, F], F32R)
        w1_hi = sb("w1_hi", [P, KC, F], F32R)
        w1_lo = sb("w1_lo", [P, KC, F], F32R)
        wq0_hi = sb("wq0_hi", [P, KC, F], F32R)
        wq0_lo = sb("wq0_lo", [P, KC, F], F32R)
        w2_hi = sb("w2_hi", [P, KC, F], F32R)
        w2_lo = sb("w2_lo", [P, KC, F], F32R)
        g_hi = sb("g_hi", [P, B, KC, HM], F32R)
        g_lo = sb("g_lo", [P, B, KC, HM], F32R)
        cols_sb = sb("cols_sb", [P, NCOLS])
        ident = sb("ident", [P, P])
        ones = sb("ones", [P, P])
        x20_sb = sb("x20_sb", [N20, F])
        vcq = sb("vcq", [P, 2 * KC, N20 + B])
        vcq2 = sb("vcq2", [P, 2 * KC, 2, N20 + B], F32R)
        rows_a = sb("rows_a", [2 * (N20 + B), ND, F])
        rows_q = sb("rows_q", [2 * (B + 1), ND, F])
        adders = {n: sb(f"adder{n}", [2 * n, n]) for n in (N20 + B, N20, B + 1)}
        crow = sb("crow", [B + 1, F])
        z20 = sb("z20", [P, N20])
        s20T = sb("s20T", [P, KC, N20 + B + 1])
        keys2 = sb("keys2", [P, KC, 2, N20], F32R)
        consts2 = sb("consts2", [P, KC, 2, B + 1], F32R)
        keyblk = sb("keyblk", [P, ND * KC, B, 4, NG])
        qc = sb("qc", [P, ND * KC, B + 1])
        rep = sb("rep", [P, B, HM], F32R)
        vblk = sb("vblk", [P, B, F])
        bout_sb = sb("bout_sb", [B + 1, ND, F])
        m_sb = sb("m_sb", [P, ND * KC, F])

        def in_g(t, part):
            return t[:, part, :, :].rearrange("p c n -> p (c n)")[:, 0:KC * F].rearrange("p (c n) -> p c n", c=KC)

        gc_hi, gc_lo = (t[0:B + 1, :, :].rearrange("p a b -> p (a b)")[:, 0:B * HM]
                        .rearrange("p (b n) -> p b n", b=B) for t in (w1_hi, w1_lo))
        wq_hi, wq_lo = (wq0_hi, in_g(g_hi, 0)), (wq0_lo, in_g(g_lo, 0))
        wk_hi, wk_lo = (in_g(g_hi, 1), w2_hi), (in_g(g_lo, 1), w2_lo)
        wo_hi, wo_lo = (wq0_hi, w2_hi), (wq0_lo, w2_lo)
        m_flat = m_sb[:, :, :].rearrange("p a b -> p (a b)")
        rep_f = m_flat[:, 0:HM]
        logit = m_flat[:, 0:HM]
        expd = m_flat[:, HM:2 * HM]
        wT = m_flat[:, 2 * HM:2 * HM + NB * P]
        outb = m_flat[:, 2 * HM + NB * P:2 * HM + NB * P + 2 * F].rearrange("p (s n) -> p s n", s=2)

        xT_sb = sb("xT_sb", [P, TPG, KC, P])
        xh = sb("xh", [P, TPG, KC, P], F32R)
        xl = sb("xl", [P, TPG, KC, P], F32R)
        x_sb = sb("x_sb", [P, TPG, F])
        rowsum = sb("rowsum", [P, TPG])
        rs_junk = sb("rs_junk", [P, F])
        adj_sb = sb("adj_sb", [P, TPG, L, DM], I32)
        vb = sb("vb", [P, TPG, DM])
        cond = sb("cond", [P, TPG, DM])
        negvb = sb("negvb", [P, TPG, DM])
        cap = sb("cap", [P, TPG, DM])
        vbn = sb("vbn", [P, TPG, P])
        vbT = sb("vbT", [P, 2, P], F32R)
        mx = sb("mx", [P, H * ND])
        den = sb("den", [P, H * ND])
        rden = sb("rden", [P, H * ND])
        w = sb("w", [P, NB, P])

        def ps(name, shape):
            return ctx.enter_context(nc.psum_tensor(name, shape, F32))

        lgP = ps("lgP", [P, 2, 512])
        outP = [ps("outP0", [P, 512]), ps("outP1", [P, 512])]
        trP = ps("trP", [P, 2, 512])
        auxP = [ps("auxP0", [P, 512]), ps("auxP1", [P, 512])]
        foldP = [lgP[:, 0, :], lgP[:, 1, :], outP[1][:, :], outP[0][:, :]]

        x20_in, cols_in, bout_in = sem("x20_in"), sem("cols_in"), sem("bout_in")
        raw_in, part_hi, part_lo = sems("raw_in", SLOTS), sem("part_hi"), sem("part_lo")
        adders_ready = sem("adders_ready")
        consts_ready, keyblk_zeroed, bout_zeroed = sem("consts_ready"), sem("keyblk_zeroed"), sem("bout_zeroed")
        vbn_set, w_set, vblk_zeroed = sem("vbn_set"), sem("w_set"), sem("vblk_zeroed")
        x20T_done, vcqx_ready, sum20_done, z20_ready, vcq_ready = (
            sem("x20T_done"), sem("vcqx_ready"), sem("sum20_done"), sem("z20_ready"), sem("vcq_ready"))
        s20_done, s20_copied = sem("s20_done"), sem("s20_copied")
        s20T_done, s20T_ready, s20T_split = sem("s20T_done"), sem("s20T_ready"), sem("s20T_split")
        qrow_done, qrow_ready, krow_done, krow_ready = (
            sem("qrow_done"), sem("qrow_ready"), sem("krow_done"), sem("krow_ready"))
        m_done, m_ready = sem("m_done"), sem("m_ready")
        k_done, key_ready, qc_done, qc_ready = sem("k_done"), sem("key_ready"), sem("qc_done"), sem("qc_ready")
        fold_done, fold_hi, fold_lo = sem("fold_done"), sem("fold_hi"), sem("fold_lo")
        v_done, v_ready, crow_done, crow_ready = sem("v_done"), sem("v_ready"), sem("crow_done"), sem("crow_ready")
        vblk_in, rep_in, rep_ready, rep_step = sem("vblk_in"), sem("rep_in"), sem("rep_ready"), sem("rep_step")
        vb01_done, vb01_ready, vbT_ready = sem("vb01_done"), sem("vb01_ready"), sem("vbT_ready")
        vb_placed = sem("vb_placed")

        xT_in, x_in = sems("xT_in", TPG), sems("x_in", TPG)
        adj_in, adj_used = sem("adj_in"), sem("adj_used")
        xh_ready, xl_ready, rowsum_ready, z_ready = sem("xh_ready"), sem("xl_ready"), sem("rowsum_ready"), sem("z_ready")
        vb_step, vb_ready, cap_ready = sem("vb_step"), sem("vb_ready"), sem("cap_ready")
        lg_done, self_done = sem("lg_done"), sems("self_done", TPG)
        masked, max_ready, shifted, exp_ready = sem("masked"), sem("max_ready"), sem("shifted"), sem("exp_ready")
        den_ready, rden_ready, w_ready = sem("den_ready"), sem("rden_ready"), sem("w_ready")
        tr_done, tr_copied = sem("tr_done"), sem("tr_copied")
        pv_done, fin_ready, stored = sem("pv_done"), sem("fin_ready"), sems("stored", 2)

        W_STEPS = 3
        VB_PLACED = 2
        TR_COPIES = 2
        VB_STEPS = L + 3
        LABELS = (0, 3, 9, L)

        def raw(n):
            s = n % SLOTS
            t = xT_sb[:, :, :, :].rearrange("p a b c -> p a (b c)") if s < TPG else x_sb[:, :, :]
            return t[:, s % TPG, :]

        def chunks(dram, hi, lo):
            return [(dram[a * P:(a + 1) * P, :], hi[:, a, :], lo[:, a, :]) for a in range(KC)]

        w1_pieces, wq0_pieces = chunks(w1, w1_hi, w1_lo), chunks(wqT[0], wq_hi[0], wq_lo[0])
        pieces = [piece for pair in zip(w1_pieces, wq0_pieces) for piece in pair]
        pieces += chunks(wselfT[0:F], ws_hi, ws_lo) + chunks(wselfT[F:2 * F], w2_hi, w2_lo)
        WS_PARTS = len(pieces)
        pieces += chunks(wqT[1], wq_hi[1], wq_lo[1])
        WQ1_PARTS = len(pieces)
        pieces += chunks(wkT[0], wk_hi[0], wk_lo[0])
        WK0_PARTS = len(pieces)
        pieces += chunks(wkT[1], wk_hi[1], wk_lo[1])
        WK1_PARTS = len(pieces)
        pieces += chunks(woT[0], wo_hi[0], wo_lo[0])
        WO0_PARTS = len(pieces)
        pieces += chunks(woT[1], wo_hi[1], wo_lo[1])

        def slot_of(i, k):
            return i + k // TPG, k % TPG

        def free(eng, s, n):
            if not (isinstance(n, int) and n <= 0):
                eng.wait_ge(s, n)

        folds = [(ic, c) for ic in (0, KC, *range(1, KC)) for c in range(KC)]
        MIDDLE = 7
        vb01P = trP[:, 0, 256:256 + 2 * P]

        block = ctx.enter_context(nc.Block())

        @block.sync
        def _(sp):
            for n, (src, _, _) in enumerate(pieces):
                if n >= SLOTS:
                    sp.wait_ge(part_lo, n - SLOTS + 1)
                sp.dma_start(raw(n), src).then_inc(raw_in[n % SLOTS], 16)
                if n == 1:
                    sp.dma_start(x20_sb[:, :], x20).then_inc(x20_in, 16)
                    sp.dma_start(cols_sb[:, :], cols).then_inc(cols_in, 16)
                if n == WK0_PARTS:
                    sp.dma_start(adj_sb[:, :, :, :], adj[0]).then_inc(adj_in, 16)
                    sp.wait_ge(bout_zeroed, 1)
                    sp.dma_start(bout_sb[B:B + 1, :, :], bout).then_inc(bout_in, 16)
            sp.wait_ge(part_lo, len(pieces))
            for k in range(TPG):
                sp.dma_start(xT_sb[:, k, :, :], xT[0, k]).then_inc(xT_in[k], 16)
                sp.dma_start(x_sb[:, k, :], x[0, k]).then_inc(x_in[k], 16)
            sp.wait_ge(vblk_zeroed, 1)
            sp.wait_ge(crow_ready, 2)
            for b in range(B):
                sp.dma_start(vblk[Z_ROW:Z_ROW + 1, b, :], crow[b:b + 1, :]).then_inc(vblk_in, 16)
                sp.dma_start(vblk[Z_ROW + 1:Z_ROW + 2, b, :], crow[B:B + 1, :]).then_inc(vblk_in, 16)

            sp.wait_ge(fold_hi, 2 * KC)
            sp.wait_ge(fold_lo, 2 * KC)
            sp.wait_ge(rep_ready, 2)
            for r, part in enumerate((gc_hi, gc_lo)):
                for b in range(B):
                    sp.dma_start(rep[VB_Z + r:VB_Z + r + 1, b, :].bitcast(F32), part[b:b + 1, b, :].bitcast(F32))\
                        .then_inc(rep_in, 16)
                sp.dma_start(rep[VB_Z + 2 + r:VB_Z + 3 + r, :, :].bitcast(F32), part[B:B + 1, :, :].bitcast(F32))\
                    .then_inc(rep_in, 16)
            for d in range(ND):
                sp.wait_ge(v_ready, d + 1)
                for b in range(B):
                    for j in range(HPG):
                        r = slice(j * DM + d * NG, j * DM + (d + 1) * NG)
                        sp.dma_start(vblk[r, b, :].rearrange("p (h n) -> p h n", n=DH)[:, j::HPG, :],
                                     rows_a[b * NG:(b + 1) * NG, d, :].rearrange("p (h n) -> p h n", n=DH)[:, j::HPG, :])\
                            .then_inc(vblk_in, 16)

            sp.wait_ge(adj_used, 1)
            sp.dma_start(adj_sb[:, :, :, :], adj[1]).then_inc(adj_in, 16)

            def turn(i, more, more_adj):
                for k in range(TPG):
                    if more:
                        sp.wait_ge(xl_ready, TPG * i + k + 1)
                        sp.dma_start(xT_sb[:, k, :, :], xT[i + 1, k]).then_inc(xT_in[k], 16)
                    sp.wait_ge(fin_ready, TPG * i + k + 1)
                    sp.dma_start(out[i, k], outb[:, k % 2, :]).then_inc(stored[k % 2], 16)
                    if more:
                        sp.dma_start(x_sb[:, k, :], x[i + 1, k]).then_inc(x_in[k], 16)
                    if more_adj and k == TPG - 2:
                        sp.wait_ge(adj_used, i + 2)
                        sp.dma_start(adj_sb[:, :, :, :], adj[i + 2]).then_inc(adj_in, 16)

            turn(0, True, True)
            with sp.Fori(1, G - 2) as i:
                turn(i, True, True)
            turn(G - 2, True, False)
            turn(G - 1, False, False)
            for s in range(2):
                sp.wait_ge(stored[s], 16 * G * TPG // 2)

        @block.tensor
        def _(pe):
            def mm(o, a, b, start, stop):
                return nc.tensor.matmul(o, a, b, start=start, stop=stop, skip_group_check=True)

            def passes(o, pairs):
                for n, (a_hi, a_lo, b_hi, b_lo) in enumerate(pairs):
                    mm(o, a_hi, b_hi, n == 0, False)
                    mm(o, a_hi, b_lo, False, False)
                    last = mm(o, a_lo, b_hi, False, n == len(pairs) - 1)
                return last

            def fold_w(d, c):
                n = d * KC + c
                cs = slice(c * P, (c + 1) * P)
                passes(foldP[n % 4], [(wq_hi[d][:, f, cs], wq_lo[d][:, f, cs], w1_hi[:, f, :], w1_lo[:, f, :])
                                      for f in range(KC)]).then_inc(m_done, 1)

            def both_parts(o, pairs):
                for n, (a, b_hi, b_lo) in enumerate(pairs):
                    mm(o, a, b_hi, n == 0, False)
                    last = mm(o, a, b_lo, False, n == len(pairs) - 1)
                return last

            def turn_and_add(o, rows, n):
                return mm(o, rows, adders[n][:, :], True, True)

            def q_rows(d):
                if d:
                    pe.wait_ge(qrow_ready, d)
                both_parts(auxP[1][0:2 * (B + 1), :], [(consts2[:, f, :, :], wq_hi[d][:, f, :], wq_lo[d][:, f, :])
                                                       for f in range(KC)]).then_inc(qrow_done, 1)

            for f in range(KC):
                for j, (wq, w1_part, parts, count) in enumerate((
                        (wq_hi[0], w1_hi, part_hi, 2 * f + 2),
                        (wq_hi[0], w1_lo, part_lo, 2 * f + 1),
                        (wq_lo[0], w1_hi, part_lo, 2 * f + 2))):
                    pe.wait_ge(parts, count)
                    for c in range(KC):
                        last = mm(foldP[c], wq[:, f, c * P:(c + 1) * P], w1_part[:, f, :],
                                  f == 0 and j == 0, f == KC - 1 and j == 2)
                        if f == KC - 1 and j == 2:
                            last.then_inc(m_done, 1)
                if f == 0:
                    pe.wait_ge(x20_in, 16)
                    pe.wait_ge(consts_ready, 3)
                    for c in range(KC):
                        last = nc.tensor.transpose(auxP[0][:, c * N20:(c + 1) * N20], x20_sb[:, c * P:(c + 1) * P],
                                                   ident[0:N20, 0:N20])
                    last.then_inc(x20T_done, 1)
                if f == KC - 2:
                    pe.wait_ge(vcqx_ready, 2)
                    for c in range(KC):
                        last = mm(auxP[1][:, 0:N20], ones[:, :], vcq[:, c, 0:N20], c == 0, c == KC - 1)
                    last.then_inc(sum20_done, 1)
            pe.wait_ge(vcq_ready, 4)
            pe.wait_ge(part_lo, WS_PARTS)
            both_parts(trP[0:2 * (N20 + B), 0, :], [(vcq2[:, c, :, :], h[:, c % KC, :], lo[:, c % KC, :])
                                                    for c in range(2 * KC)
                                                    for h, lo in (((ws_hi, ws_lo), (w2_hi, w2_lo))[c // KC],)])\
                .then_inc(s20_done, 1)
            pe.wait_ge(part_lo, WQ1_PARTS)
            pe.wait_ge(m_ready, 1)
            fold_w(1, 0)
            pe.wait_ge(adders_ready, len(adders))
            pe.wait_ge(s20_copied, 1)
            for f in range(KC):
                last = turn_and_add(auxP[0][:, f * 64:f * 64 + N20 + B], rows_a[:, 0, f * P:(f + 1) * P], N20 + B)
            last.then_inc(s20T_done, 1)
            pe.wait_ge(m_ready, 2)
            fold_w(1, 1)
            pe.wait_ge(s20T_split, 4)
            q_rows(0)
            pe.wait_ge(m_ready, 3)
            fold_w(1, 2)
            pe.wait_ge(part_lo, WK1_PARTS)
            for d in range(ND):
                both_parts(trP[0:2 * N20, d, :], [(keys2[:, f, :, :], wk_hi[d][:, f, :], wk_lo[d][:, f, :])
                                                  for f in range(KC)]).then_inc(krow_done, 1)
            pe.wait_ge(m_ready, 4)
            fold_w(1, 3)
            pe.wait_ge(krow_ready, ND)
            for n in range(ND * KC):
                last = turn_and_add(auxP[0][:, n * N20:(n + 1) * N20],
                                    rows_a[0:2 * N20, n // KC, n % KC * P:(n % KC + 1) * P], N20)
            last.then_inc(k_done, 1)
            for f in range(KC):
                last = nc.tensor.transpose(trP[0:B + 1, 1, f * P:(f + 1) * P], s20T[:, f, N20:N20 + B + 1], ident[:, :])
            last.then_inc(crow_done, 1)
            q_rows(1)
            pe.wait_ge(m_ready, ND * KC)
            pe.wait_ge(key_ready, 4)
            for n, (ic, c) in enumerate(folds):
                if n >= 4:
                    pe.wait_ge(fold_hi, n - 3)
                    pe.wait_ge(fold_lo, n - 3)
                if n == KC:
                    pe.wait_ge(qc_ready, 2)
                for d in range(ND):
                    if ic < KC:
                        o, a = foldP[n % 4], m_sb[:, d * KC + c, ic * P:(ic + 1) * P]
                    else:
                        o, a = foldP[n % 4][0:B + 1], qc[:, d * KC + c, :]
                    o = o[:, 0:B * 4 * DM].rearrange("p (b h n) -> p b h n", b=B, h=4)[:, :, :, d * NG:(d + 1) * NG]
                    last = mm(o, a, keyblk[:, d * KC + c, :, :, :], d == 0, d == 1)
                last.then_inc(fold_done, 1)
                if n == 0:
                    pe.wait_ge(qrow_ready, ND)
                    for j in range(ND * KC):
                        last = turn_and_add(trP[:, 0, j * 4:j * 4 + B + 1],
                                            rows_q[:, j // KC, j % KC * P:(j % KC + 1) * P], B + 1)
                    last.then_inc(qc_done, 1)
                if n == MIDDLE:
                    pe.wait_ge(part_lo, len(pieces))
                    for d in range(ND):
                        passes(auxP[d][0:N20, :], [(keys2[:, f, 0, :], keys2[:, f, 1, :],
                                                    wo_hi[d][:, f, :], wo_lo[d][:, f, :]) for f in range(KC)])\
                            .then_inc(v_done, 1)
                    pe.wait_ge(vb_ready, 1)
                    pe.wait_ge(z_ready, 2)
                    for k in range(2):
                        last = nc.tensor.transpose(vb01P[:, k * P:(k + 1) * P], vbn[:, k, :], ident[:, :])
                    last.then_inc(vb01_done, 1)

            def logits(i, k, b, first=False):
                t = TPG * i + k
                pe.wait_ge(xh_ready, t + 1)
                pe.wait_ge(xl_ready, t + 1)
                free(pe, masked, t)
                s = k % TPG
                for c in range(KC):
                    if first and c == KC - 1:
                        pe.wait_ge(fold_hi, len(folds))
                        pe.wait_ge(fold_lo, len(folds))
                    for a, g in ((xh, g_hi), (xh, g_lo), (xl, g_hi)):
                        for h in range(2):
                            mm(lgP[:, h, 0:HALF], a[:, s, c, :], g[:, b, c, h * HALF:(h + 1) * HALF],
                               c == 0 and a is xh and g is g_hi, False)
                if first:
                    pe.wait_ge(rep_in, 16 * 2 * (B + 1))
                else:
                    free(pe, vbT_ready, t - 1)
                for h in range(2):
                    last = mm(lgP[:, h, 0:HALF], vbT[0:VB_K, k % 2, :], rep[0:VB_K, b, h * HALF:(h + 1) * HALF],
                              False, True)
                last.then_inc(lg_done, 1)

            def self_rows(i, k):
                t = TPG * i + k
                s = k % TPG
                free(pe, fin_ready, t - 1)
                for c in range(KC):
                    for a, g in ((xh, ws_hi), (xh, ws_lo), (xl, ws_hi)):
                        last = mm(outP[k % 2][:, :], a[:, s, c, :], g[:, c, :],
                                  c == 0 and a is xh and g is ws_hi, False)
                last.then_inc(self_done[s], 1)

            def turned(i, k, vb_next, vb_before):
                t = TPG * i + k
                pe.wait_ge(w_ready, W_STEPS * t + 2)
                free(pe, tr_copied, TR_COPIES * t)
                for e in range(NB):
                    if e == NB - 1:
                        pe.wait_ge(w_ready, W_STEPS * t + W_STEPS)
                        if vb_next:
                            pe.wait_ge(vb_placed, VB_PLACED * t + VB_PLACED)
                        if vb_before:
                            free(pe, vbT_ready, t)
                    last = nc.tensor.transpose(trP[:, e // 4, (e % 4) * P:(e % 4 + 1) * P], w[:, e, :], ident[:, :])
                last.then_inc(tr_done, 1)

            def values(i, k, b):
                t = TPG * i + k
                pe.wait_ge(tr_copied, TR_COPIES * t + 1)
                for e in range(NB):
                    if e == 4:
                        pe.wait_ge(tr_copied, TR_COPIES * t + TR_COPIES)
                    n = min(BF, F - e * BF)
                    last = mm(outP[k % 2][:, e * BF:e * BF + n], wT[:, e * P:(e + 1) * P],
                              vblk[:, b, e * BF:e * BF + n], False, e == NB - 1)
                last.then_inc(pv_done, 1)

            pe.wait_ge(fold_hi, len(folds) - 2)
            pe.wait_ge(fold_lo, len(folds) - 2)
            pe.wait_ge(vb01_ready, 1)
            logits(0, 0, 0, first=True)
            self_rows(0, 0)
            pe.wait_ge(vblk_in, 16 * (B * ND * HPG + 2 * B))

            def step(i, k):
                following = (i, k + 1) if k + 1 < TPG else (i + 1, 0)
                logits(*following, following[0] // GPB)
                turned(i, k, vb_next=True, vb_before=True)
                self_rows(*following)
                values(i, k, i // GPB)

            def turn(i):
                for k in range(TPG):
                    step(i, k)

            turn(0)
            with pe.Fori(1, G - 1) as i:
                turn(i)
            i, b = G - 1, B - 1
            for k in range(TPG - 3):
                step(i, k)
            logits(i, TPG - 2, b)
            turned(i, TPG - 3, vb_next=True, vb_before=True)
            logits(i, TPG - 1, b)
            values(i, TPG - 3, b)
            for k in (TPG - 2, TPG - 1):
                turned(i, k, vb_next=False, vb_before=k == TPG - 2)
                self_rows(i, k)
                values(i, k, b)

        @block.scalar
        def _(act):
            def split_hi(i, k):
                i2, s = slot_of(i, k)
                act.wait_ge(xT_in[s], 16 * i2 + 16)
                free(act, self_done[s], i2)
                nc.scalar.activation(xh[:, s, :, :], xT_sb[:, s, :, :], ACT.Copy).then_inc(xh_ready, 1)
                act.wait_ge(x_in[s], 16 * i2 + 16)
                free(act, rowsum_ready, TPG * i + k)
                nc.scalar.activation(rs_junk[:, :], x_sb[:, s, :], ACT.Copy,
                                     accum_out=rowsum[:, s:s + 1]).then_inc(rowsum_ready, 1)

            def upper(first, end):
                for n in range(first, end):
                    act.wait_ge(raw_in[n % SLOTS], 16 * (n // SLOTS) + 16)
                    nc.scalar.activation(pieces[n][1], raw(n), ACT.Copy).then_inc(part_hi, 1)

            def copy_m(n):
                act.wait_ge(m_done, n + 1)
                nc.scalar.activation(m_sb[:, n, :], foldP[n % 4], ACT.Copy).then_inc(m_ready, 1)

            def copy_q(d):
                act.wait_ge(qrow_done, d + 1)
                nc.scalar.activation(rows_q[:, d, :], auxP[1][0:2 * (B + 1), :], ACT.Copy).then_inc(qrow_ready, 1)

            upper(0, WQ1_PARTS)
            act.wait_ge(rep_ready, 2)
            copy_m(0)
            copy_m(1)
            upper(WQ1_PARTS, WK0_PARTS)
            copy_m(2)
            copy_m(3)
            act.wait_ge(s20_done, 1)
            nc.scalar.activation(rows_a[:, 0, :], trP[0:2 * (N20 + B), 0, :], ACT.Copy).then_inc(s20_copied, 1)
            upper(WK0_PARTS, WK1_PARTS)
            copy_m(4)
            copy_m(5)
            copy_q(0)
            upper(WK1_PARTS, WO0_PARTS)
            copy_m(6)
            for d in range(ND):
                act.wait_ge(krow_done, d + 1)
                nc.scalar.activation(rows_a[0:2 * N20, d, :], trP[0:2 * N20, d, :], ACT.Copy).then_inc(krow_ready, 1)
            upper(WO0_PARTS, len(pieces))
            copy_m(7)
            copy_q(1)
            act.wait_ge(k_done, 1)
            for n, (ic, c) in enumerate(folds):
                act.wait_ge(fold_done, n + 1)
                if ic < KC:
                    o, a = g_hi[:, :, ic, :], foldP[n % 4]
                else:
                    o, a = gc_hi, foldP[n % 4][0:B + 1]
                nc.scalar.activation(o[:, :, c * 4 * DM:(c + 1) * 4 * DM].bitcast(F32R),
                                     a[:, 0:B * 4 * DM].rearrange("p (b n) -> p b n", b=B),
                                     ACT.Copy, scale=SCALE).then_inc(fold_hi, 1)
                if n == MIDDLE:
                    split_hi(0, 0)
                    split_hi(0, 1)
                    for d in range(ND):
                        act.wait_ge(v_done, d + 1)
                        nc.scalar.activation(rows_a[0:N20, d, :], auxP[d][0:N20, :], ACT.Copy).then_inc(v_ready, 1)
                    act.wait_ge(vb01_done, 1)
                    nc.scalar.activation(vbT[:, :, :], vb01P.rearrange("p (s n) -> p s n", s=2), ACT.Copy)\
                        .then_inc(vb01_ready, 1)
            split_hi(0, 2)

            def exponentials(i, k):
                t = TPG * i + k
                act.wait_ge(shifted, t + 1)
                free(act, w_ready, W_STEPS * t)
                nc.scalar.activation(expd, logit, ACT.Exp).then_inc(exp_ready, 1)

            exponentials(0, 0)

            def turn(i, last):
                for k in range(TPG):
                    t = TPG * i + k
                    act.wait_ge(tr_done, t + 1)
                    free(act, pv_done, t)
                    nc.scalar.activation(wT[:, 0:4 * P], trP[:, 0, :], ACT.Copy).then_inc(tr_copied, 1)
                    nc.scalar.activation(wT[:, 4 * P:NB * P], trP[:, 1, 0:2 * P], ACT.Copy).then_inc(tr_copied, 1)
                    if not (last and k >= TPG - 2):
                        act.wait_ge(lg_done, t + 1)
                        nc.scalar.activation(vbT[:, k % 2, :], trP[:, 1, P:2 * P], ACT.Copy).then_inc(vbT_ready, 1)
                    if not (last and k >= TPG - 1):
                        exponentials(*((i, k + 1) if k + 1 < TPG else (i + 1, 0)))
                    if not (last and k >= TPG - 3):
                        split_hi(i, k + 3)

            turn(0, False)
            with act.Fori(1, G - 1) as i:
                turn(i, False)
            turn(G - 1, True)

        @block.vector
        def _(dve):
            nc.vector.memset(vcq[:, 0:KC, N20:N20 + B], 0.0).then_inc(vcqx_ready, 1)
            nc.vector.memset(keyblk[:, :, :, :, :], 0.0).then_inc(keyblk_zeroed, 1)

            def lower(first, end):
                for n in range(first, end):
                    dve.wait_ge(part_hi, n + 1)
                    nc.vector.tensor_tensor(pieces[n][2], raw(n), pieces[n][1].bitcast(F32), ALU.subtract)\
                        .then_inc(part_lo, 1)

            lower(0, 2 * KC)
            dve.wait_ge(x20T_done, 1)
            nc.vector.tensor_copy(vcq[:, 0:KC, 0:N20], auxP[0][:, 0:KC * N20].rearrange("p (c n) -> p c n", c=KC))\
                .then_inc(vcqx_ready, 1)
            lower(2 * KC, WS_PARTS)
            dve.wait_ge(sum20_done, 1)
            nc.vector.tensor_scalar(z20[:, :], auxP[1][:, 0:N20], 0.0, None, ALU.not_equal).then_inc(z20_ready, 1)
            dve.wait_ge(cols_in, 16)
            q_cols = cols_sb[:, C_Q:C_Q + KC * B].rearrange("p (c b) -> p c b", b=B)
            dve.wait_ge(z20_ready, 1)
            nc.vector.tensor_tensor(
                vcq[:, KC:2 * KC, 0:N20].rearrange("p c (b m) -> p c b m", b=B),
                z20[:, :].rearrange("p (b m) -> p b m", b=B).unsqueeze(1).to_broadcast([P, KC, B, NG]),
                q_cols.unsqueeze(3).to_broadcast([P, KC, B, NG]), ALU.mult).then_inc(vcq_ready, 1)
            nc.vector.tensor_copy(vcq[:, KC:2 * KC, N20:N20 + B], q_cols).then_inc(vcq_ready, 1)
            dve.wait_ge(vcq_ready, 2)
            nc.vector.tensor_copy(vcq2[:, :, 0, :], vcq[:, :, :]).then_inc(vcq_ready, 1)
            dve.wait_ge(vcq_ready, 3)
            nc.vector.tensor_tensor(vcq2[:, :, 1, :], vcq[:, :, :], vcq2[:, :, 0, :].bitcast(F32), ALU.subtract)\
                .then_inc(vcq_ready, 1)
            lower(WS_PARTS, WK0_PARTS)
            b_self = cols_sb[:, C_BSELF:C_BSELF + KC]
            nc.vector.tensor_copy(s20T[:, :, N20 + B:N20 + B + 1], b_self.unsqueeze(2)).then_inc(s20T_ready, 1)
            dve.wait_ge(s20T_done, 1)
            s20P = auxP[0][:, 0:KC * 64].rearrange("p (c n) -> p c n", c=KC)
            nc.vector.tensor_copy(s20T[:, :, N20:N20 + B], s20P[:, :, N20:N20 + B]).then_inc(s20T_ready, 1)
            nc.vector.tensor_tensor(s20T[:, :, 0:N20], s20P[:, :, 0:N20],
                                    b_self.unsqueeze(2).to_broadcast([P, KC, N20]), ALU.add).then_inc(s20T_ready, 1)
            dve.wait_ge(s20T_ready, 3)
            nc.vector.tensor_copy(keys2[:, :, 0, :], s20T[:, :, 0:N20]).then_inc(s20T_split, 1)
            nc.vector.tensor_copy(consts2[:, :, 0, :], s20T[:, :, N20:]).then_inc(s20T_split, 1)
            dve.wait_ge(s20T_split, 2)
            nc.vector.tensor_tensor(keys2[:, :, 1, :], s20T[:, :, 0:N20], keys2[:, :, 0, :].bitcast(F32),
                                    ALU.subtract).then_inc(s20T_split, 1)
            nc.vector.tensor_tensor(consts2[:, :, 1, :], s20T[:, :, N20:], consts2[:, :, 0, :].bitcast(F32),
                                    ALU.subtract).then_inc(s20T_split, 1)
            lower(WK0_PARTS, WK1_PARTS)

            adj_l = [adj_sb[:, :, j, :] for j in range(L)]
            w_bias = [cols_sb[:, C_WB + j:C_WB + j + 1] for j in range(L)]

            def link(ins, i, step):
                ins.then_inc(vb_step, 1)
                dve.wait_ge(vb_step, VB_STEPS * i + step)

            def edge_bias(i, first, end):
                if first == 0:
                    dve.wait_ge(adj_in, 16 * i + 16)
                    link(nc.vector.tensor_scalar(vb[:, :, :], adj_l[0], w_bias[0], cols_sb[:, C_BB:C_BB + 1],
                                                 ALU.mult, ALU.add), i, 1)
                for j in range(max(first, 1), end):
                    link(nc.vector.scalar_tensor_tensor(vb[:, :, :], adj_l[j], w_bias[j], vb[:, :, :],
                                                        ALU.mult, ALU.add), i, j + 1)

            def edge_rows(i):
                link(nc.vector.tensor_copy(vbn[:, :, VB_0:VB_0 + DM].bitcast(F32R), vb[:, :, :]), i, L + 1)
                nc.vector.tensor_tensor(vbn[:, :, VB_0 + DM:VB_0 + 2 * DM].bitcast(F32R), vb[:, :, :],
                                        vbn[:, :, VB_0:VB_0 + DM],
                                        ALU.subtract).then_inc(vb_ready, 1)

            def edge_cap(i):
                ins = nc.vector.tensor_reduce(cond[:, :, :], adj_sb[:, :, :, :].rearrange("p t l m -> p t m l"),
                                              AX_X, ALU.add)
                link(ins, i, L + 2)
                nc.vector.tensor_scalar(negvb[:, :, :], vb[:, :, :], NEG, None, ALU.add).then_inc(adj_used, 1)

            def edge_cap_in(i):
                link(nc.vector.tensor_scalar(cond[:, :, :], cond[:, :, :], 0.0, HUGE, ALU.is_gt, ALU.mult), i, L + 3)
                dve.wait_ge(adj_used, i + 1)
                nc.vector.tensor_tensor(cap[:, :, :], negvb[:, :, :], cond[:, :, :], ALU.add).then_inc(cap_ready, 1)

            def row_flags(i, k):
                i2, s = slot_of(i, k)
                dve.wait_ge(rowsum_ready, TPG * i + k + 1)
                nc.vector.tensor_scalar(vbn[:, s, VB_Z:VB_Z + 2], rowsum[:, s:s + 1].to_broadcast([P, 2]),
                                        0.0, None, ALU.not_equal).then_inc(z_ready, 1)

            def shift(i, k):
                t = TPG * i + k
                dve.wait_ge(lg_done, t + 1)
                dve.wait_ge(cap_ready, i + 1)
                nc.vector.tensor_tensor(
                    logit.rearrange("p (a h n) -> p a h n", a=2, n=DM),
                    lgP[:, :, 0:HALF].rearrange("p a (h n) -> p a h n", n=DM),
                    cap[:, k, :].unsqueeze(1).unsqueeze(1).to_broadcast([P, 2, H // 2, DM]),
                    ALU.min).then_inc(masked, 1)
                dve.wait_ge(masked, t + 1)
                soft = logit.rearrange("p (g m) -> p g m", m=NG)
                nc.vector.tensor_reduce(mx[:, :], soft, AX_X, ALU.max).then_inc(max_ready, 1)
                dve.wait_ge(max_ready, t + 1)
                nc.vector.tensor_tensor(soft, soft, mx[:, :].unsqueeze(2).to_broadcast([P, H * ND, NG]),
                                        ALU.subtract).then_inc(shifted, 1)

            def weigh(i, k, flags=None):
                t = TPG * i + k
                free(dve, tr_done, t)
                nc.vector.tensor_scalar(w[:, :, Z_ROW:Z_ROW + 1], rowsum[:, k:k + 1].unsqueeze(1)
                                        .to_broadcast([P, NB, 1]), 0.0, None, ALU.not_equal).then_inc(w_ready, 1)
                dve.wait_ge(exp_ready, t + 1)
                nc.vector.tensor_reduce(den[:, :], expd.rearrange("p (g m) -> p g m", m=NG), AX_X, ALU.add)\
                    .then_inc(den_ready, 1)
                dve.wait_ge(den_ready, t + 1)
                nc.vector.reciprocal(rden[:, :], den[:, :]).then_inc(rden_ready, 1)
                if flags:
                    row_flags(*flags)
                dve.wait_ge(rden_ready, t + 1)
                full = (NB - 1) * BK
                nf = full // NG
                nc.vector.tensor_tensor(
                    w[:, 0:NB - 1, 0:BK].rearrange("p e (g m) -> p e g m", m=NG),
                    expd[:, 0:full].rearrange("p (e g m) -> p e g m", e=NB - 1, m=NG),
                    rden[:, 0:nf].rearrange("p (e g) -> p e g", e=NB - 1).unsqueeze(3)
                    .to_broadcast([P, NB - 1, BK // NG, NG]), ALU.mult).then_inc(w_ready, 1)
                nc.vector.tensor_tensor(
                    w[:, NB - 1, 0:HM - full].rearrange("p (g m) -> p g m", m=NG),
                    expd[:, full:HM].rearrange("p (g m) -> p g m", m=NG),
                    rden[:, nf:].unsqueeze(2).to_broadcast([P, H * ND - nf, NG]), ALU.mult).then_inc(w_ready, 1)

            def finish(i, k):
                t = TPG * i + k
                dve.wait_ge(pv_done, t + 1)
                dve.wait_ge(x_in[k], 16 * i + 16)
                free(dve, stored[k % 2], 16 * (2 * i + k // 2))
                nc.vector.scalar_tensor_tensor(outb[:, k % 2, :], outP[k % 2][:, :], 0.0, x_sb[:, k, :],
                                               ALU.max, ALU.add).then_inc(fin_ready, 1)

            lower(WK1_PARTS, WO0_PARTS)
            edge_bias(0, 0, L)
            dve.wait_ge(vbn_set, 4)
            edge_rows(0)
            lower(WO0_PARTS, len(pieces))
            b_k = cols_sb[:, C_BK:C_BK + ND * KC]
            kP = auxP[0][:, 0:ND * KC * N20].rearrange("p (c b m) -> p c b m", b=B, m=NG)
            dve.wait_ge(k_done, 1)
            dve.wait_ge(keyblk_zeroed, 1)
            for h in range(4):
                r = slice(h * DH, (h + 1) * DH)
                nc.vector.tensor_tensor(keyblk[r, :, :, h, :], kP[r],
                                        b_k[r].unsqueeze(2).unsqueeze(2).to_broadcast([DH, ND * KC, B, NG]),
                                        ALU.add).then_inc(key_ready, 1)
            dve.wait_ge(crow_done, 1)
            dve.wait_ge(bout_in, 16)
            nc.vector.tensor_tensor(crow[:, :], trP[0:B + 1, 1, :], bout_sb[:, 0, :], ALU.add).then_inc(crow_ready, 1)
            dve.wait_ge(crow_ready, 1)
            nc.vector.tensor_tensor(crow[:, :], crow[:, :], bout_sb[:, 1, :], ALU.add).then_inc(crow_ready, 1)
            dve.wait_ge(qc_done, 1)
            qcP = trP[:, 0, 0:ND * KC * 4].rearrange("p (c n) -> p c n", n=4)
            nc.vector.tensor_copy(qc[:, :, 0:B], qcP[:, :, 0:B]).then_inc(qc_ready, 1)
            nc.vector.tensor_tensor(qc[:, :, B:B + 1], qcP[:, :, B:B + 1],
                                    cols_sb[:, C_BQ:C_BQ + ND * KC].unsqueeze(2), ALU.add).then_inc(qc_ready, 1)
            for n, (ic, c) in enumerate(folds):
                dve.wait_ge(fold_hi, n + 1)
                if ic < KC:
                    o, hi, a = g_lo[:, :, ic, :], g_hi[:, :, ic, :], foldP[n % 4]
                else:
                    o, hi, a = gc_lo, gc_hi, foldP[n % 4][0:B + 1]
                cs = slice(c * 4 * DM, (c + 1) * 4 * DM)
                nc.vector.scalar_tensor_tensor(o[:, :, cs].bitcast(F32R),
                                               a[:, 0:B * 4 * DM].rearrange("p (b n) -> p b n", b=B),
                                               SCALE, hi[:, :, cs].bitcast(F32), ALU.mult, ALU.subtract)\
                    .then_inc(fold_lo, 1)
                if n == MIDDLE:
                    row_flags(0, 0)
                    row_flags(0, 1)
            edge_cap(0)
            edge_cap_in(0)
            shift(0, 0)
            dve.wait_ge(w_set, 2)
            weigh(0, 0, flags=(0, 2))

            def turn(i, last):
                for k in range(TPG):
                    more = not (last and k == TPG - 1)
                    if more:
                        i1, k1 = (i, k + 1) if k + 1 < TPG else (i + 1, 0)
                        shift(i1, k1)
                    if not last and k == 0:
                        edge_bias(i + 1, LABELS[0], LABELS[1])
                    if not last and k == 1:
                        edge_bias(i + 1, LABELS[2], LABELS[3])
                        dve.wait_ge(vb_placed, VB_PLACED * (TPG * i + 2))
                        edge_rows(i + 1)
                    if last and k == TPG - 2:
                        finish(i, k - 1)
                    if more:
                        weigh(i1, k1, flags=None if last and k >= TPG - 3 else (i, k + 3))
                    if not (last and k == TPG - 3):
                        finish(i, k)
                    if not last and k == 0:
                        edge_bias(i + 1, LABELS[1], LABELS[2])
                    if not last and k == 2:
                        edge_cap(i + 1)
                        edge_cap_in(i + 1)

            turn(0, False)
            with dve.Fori(1, G - 1) as i:
                turn(i, False)
            turn(G - 1, True)

        @block.gpsimd
        def _(pool):
            nc.gpsimd.memset(ident[:, :], 0.0).then_inc(consts_ready, 1)
            nc.gpsimd.memset(ones[:, :], 1.0).then_inc(consts_ready, 1)
            pool.wait_ge(consts_ready, 1)
            nc.gpsimd.affine_select(out=ident[:, :], in_=ident[:, :], compare_op=ALU.not_equal, fill=1.0, base=0,
                                    pattern=[[-1, P]], channel_multiplier=1).then_inc(consts_ready, 1)
            pool.wait_ge(consts_ready, 3)
            for n in adders:
                nc.gpsimd.tensor_tensor(adders[n][:, :], ident[0:2 * n, 0:n], ident[0:2 * n, n:2 * n], ALU.add)\
                    .then_inc(adders_ready, 1)
            nc.gpsimd.memset(bout_sb[:, :, :], 0.0).then_inc(bout_zeroed, 1)
            nc.gpsimd.memset(vbn[:, :, VB_Z:VB_K], 1.0).then_inc(vbn_set, 1)
            nc.gpsimd.memset(vbn[:, :, VB_K:P], 0.0).then_inc(vbn_set, 1)
            nc.gpsimd.memset(vbn[:, :, 0:VB_0], 0.0).then_inc(vbn_set, 1)
            nc.gpsimd.memset(vbn[:, :, Z_ROW:VB_Z], 0.0).then_inc(vbn_set, 1)
            nc.gpsimd.memset(rep_f, 0.0).then_inc(rep_step, 1)
            for part in range(2):
                pool.wait_ge(rep_step, part + 1)
                nc.gpsimd.affine_select(out=rep_f, in_=rep_f, compare_op=ALU.not_equal, fill=1.0,
                                        base=-VB_0 - part * DM, pattern=[[0, H], [-1, DM]], channel_multiplier=1)\
                    .then_inc(rep_step, 1)
            pool.wait_ge(rep_step, 3)
            for b in range(B):
                nc.gpsimd.tensor_copy(rep[:, b, :], rep_f).then_inc(rep_ready, 1)
            nc.gpsimd.memset(vblk[:, :, :], 0.0).then_inc(vblk_zeroed, 1)
            nc.gpsimd.memset(w[:, :, :], 0.0).then_inc(w_set, 1)
            pool.wait_ge(w_set, 1)
            nc.gpsimd.memset(w[:, :, Z_ROW + 1:Z_ROW + 2], 1.0).then_inc(w_set, 1)

            def split_lo(i, k):
                i2, s = slot_of(i, k)
                pool.wait_ge(xh_ready, TPG * i + k + 1)
                free(pool, self_done[s], i2)
                nc.gpsimd.tensor_tensor(xl[:, s, :, :], xT_sb[:, s, :, :], xh[:, s, :, :].bitcast(F32),
                                        ALU.subtract).then_inc(xl_ready, 1)

            def place_vb(i, k):
                t = TPG * i + k
                i2, s2 = slot_of(i, k + 2)
                free(pool, tr_done, t)
                pool.wait_ge(vb_ready, i2 + 1)
                pool.wait_ge(z_ready, t + 3)
                for cs in (slice(VB_0, VB_0 + 2 * DM), slice(VB_Z, VB_K)):
                    nc.gpsimd.tensor_tensor(w[:, NB - 1, cs], vbn[:, s2, cs], ones[:, cs], ALU.mult)\
                        .then_inc(vb_placed, 1)

            split_lo(0, 0)
            split_lo(0, 1)
            split_lo(0, 2)

            def turn(i, last):
                for k in range(TPG):
                    if not (last and k >= TPG - 2):
                        place_vb(i, k)
                    if not (last and k >= TPG - 3):
                        split_lo(i, k + 3)

            turn(0, False)
            with pool.Fori(1, G - 1) as i:
                turn(i, False)
            turn(G - 1, True)

        return nc


def kernel(**inputs):
    import numpy as np
    import concourse.bacc as bacc
    from concourse.bass_utils import run_bass_kernel_spmd

    def arr(name):
        return np.asarray(inputs[name])

    x = arr("x")
    adj = arr("mask_BxSxSx11_ik0")
    pre = "L0_cond_"
    n = x.shape[1]
    groups = B * n // (P * TPG)
    x_t = x.reshape(groups, TPG, P, F)
    xT = x_t.reshape(groups, TPG, P, KC, P).transpose(0, 1, 4, 3, 2)
    a0 = adj[:, :, :NG, :].transpose(0, 1, 3, 2)
    a1 = adj[:, :NG, :, :].transpose(0, 2, 3, 1)
    a = np.concatenate([a0, a1], axis=3).reshape(groups, TPG, P, L, DM).transpose(0, 2, 1, 3, 4)

    def columns(v):
        return v.reshape(-1, P).T

    cols = np.concatenate([
        columns(arr(pre + "b_self")), columns(arr(pre + "bq")), columns(arr(pre + "bk")),
        arr("cond_1024").reshape(B, KC, P).transpose(2, 1, 0).reshape(P, KC * B),
        np.broadcast_to(arr(pre + "w_bias"), (P, L)), np.broadcast_to(arr(pre + "b_bias"), (P, 1))], axis=1)
    w_self = arr(pre + "W_self")
    arrays = {
        "x": x_t, "xT": xT, "x20": x[:, :NG].reshape(B * NG, F), "adj": a,
        "wselfT": w_self.T, "w1": w_self[:, :F],
        "wqT": arr(pre + "Wq").transpose(0, 2, 1), "wkT": arr(pre + "Wk").transpose(0, 2, 1),
        "woT": arr(pre + "Wout").reshape(ND, F, F).transpose(0, 2, 1),
        "cols": cols, "bout": arr(pre + "bout").reshape(1, ND, F),
    }
    arrays = {k: np.ascontiguousarray(v) for k, v in arrays.items()}

    nc = bacc.Bacc("TRN2", target_bir_lowering=False, num_devices=1)
    aps = {k: nc.dram_tensor(f"in_{k}", v.shape, mybir.dt.from_np(v.dtype), kind="ExternalInput").ap()
           for k, v in arrays.items()}
    out = nc.dram_tensor("out", x_t.shape, F32, kind="ExternalOutput").ap()
    build(nc, *(aps[k] for k in arrays), out)
    r = run_bass_kernel_spmd(nc, [{f"in_{k}": v for k, v in arrays.items()}], core_ids=[0])
    return r.results[0]["out"].reshape(B, n, F)
```
